# Optimizing a Trainium2 kernel written in Bass

```python
import numpy as np
import jax
import jax.numpy as jnp

def _softmax(x, axis=-1):
    return jax.nn.softmax(x, axis=axis)

def _gelu(x):
    return jax.nn.gelu(x, approximate=True)

def _silu(x):
    return jax.nn.silu(x)

def _sigmoid(x):
    return jax.nn.sigmoid(x)

def _layernorm(x, axis=-1, eps=1e-05):
    m = jnp.mean(x, axis=axis, keepdims=True)
    v = jnp.var(x, axis=axis, keepdims=True)
    return (x - m) / jnp.sqrt(v + eps)

def _scatter_add(tgt, idx, src, axis=0):
    return tgt.at[idx].add(src)

def _segment_sum(src, seg, n):
    return jax.ops.segment_sum(src, seg, n)
kernel_name = 'mk_cond_resid_d4_seqx_r8_1381ba'

def setup_inputs(seed: int=0):
    np.random.seed(seed)
    _w = jnp.asarray

    def _rec_inputs():
        import jax
        import jax.numpy as jnp
        _rk = jax.random.key(seed)
        x = -0.000125 + 0.9999 * jax.random.normal(jax.random.fold_in(_rk, 1), (32, 128, 128), jnp.float32)
        _lenS = 128 - jax.random.randint(jax.random.fold_in(_rk, 7), (32,), 0, max(1, 128 // 4) + 1, jnp.int32)
        _lenS2 = 128 - jax.random.randint(jax.random.fold_in(_rk, 8), (32,), 0, max(1, 128 // 4) + 1, jnp.int32)
        cond_1024 = 0.00513981 + 1.0024 * jax.random.normal(jax.random.fold_in(_rk, 11), (32, 128), jnp.float32)
        return (x, cond_1024)
    x, cond_1024 = _rec_inputs()

    def _L0_cond_setup():
        import jax, jax.numpy as jnp
        import numpy as np
        IN_FEATURES = 128
        OUT_FEATURES = 128
        BATCH = 32
        SEQ = 128
        EPS = 1e-08
        key = jax.random.key(seed)
        k1, k2, k3 = jax.random.split(key, 3)
        Efou = jax.random.normal(k1, (BATCH, SEQ, IN_FEATURES), dtype=jnp.float32)
        y = jax.random.normal(k2, (BATCH, IN_FEATURES), dtype=jnp.float32)
        weight = jax.random.normal(k3, (IN_FEATURES, OUT_FEATURES), dtype=jnp.float32)
        return {'Efou': Efou, 'y': y, 'weight': weight}
    _L0_cond_all = _L0_cond_setup()
    _L0_cond_in = {k: v for k, v in _L0_cond_all.items() if k in ('weight',)}
    del _L0_cond_all

    def _L1_cond_setup():
        import jax, jax.numpy as jnp
        import numpy as np
        key = jax.random.key(seed)
        ks = jax.random.split(key, 8)
        B, L, D, N, K = (4, 512, 128, 64, 4)
        return {'x': jax.random.normal(ks[0], (B, L, D), dtype=jnp.float32), 'conv_w': jax.random.normal(ks[1], (K, 1, D), dtype=jnp.float32) * 0.1, 'conv_b': jnp.zeros((D,), dtype=jnp.float32), 'Wp': jax.random.normal(ks[2], (D, 2 * N), dtype=jnp.float32) * (1.0 / np.sqrt(D)), 'bp': jnp.zeros((2 * N,), dtype=jnp.float32), 'Ws': jax.random.normal(ks[3], (D, N), dtype=jnp.float32) * (1.0 / np.sqrt(D)), 'bs': jnp.zeros((N,), dtype=jnp.float32), 'A_log': jax.random.normal(ks[4], (N,), dtype=jnp.float32) * 0.02, 'dt_log': jax.random.normal(ks[5], (N,), dtype=jnp.float32) * 0.02, 'Wo': jax.random.normal(ks[6], (N, D), dtype=jnp.float32) * (1.0 / np.sqrt(N)), 'bo': jnp.zeros((D,), dtype=jnp.float32)}
    _L1_cond_all = _L1_cond_setup()
    _L1_cond_in = {k: v for k, v in _L1_cond_all.items() if k in ('conv_b', 'Wp', 'bp', 'Ws', 'bs', 'A_log', 'dt_log', 'Wo', 'bo')}
    del _L1_cond_all

    def _L2_cond_setup():
        import jax, jax.numpy as jnp
        import numpy as np
        LATENT = 128
        key = jax.random.key(seed)
        k1, k2, k3, k4 = jax.random.split(key, 4)
        B, T, D = (64, 64, LATENT)
        h_t = jax.random.normal(k1, (B, D), dtype=jnp.float32)
        z = jax.random.normal(k2, (B, T, D), dtype=jnp.float32)
        bound = 1.0 / np.sqrt(2 * D)
        W = jax.random.uniform(k3, (D, 2 * D), minval=-bound, maxval=bound, dtype=jnp.float32)
        b = jax.random.uniform(k4, (D,), minval=-bound, maxval=bound, dtype=jnp.float32)
        alpha = jnp.full((D,), 0.1, dtype=jnp.float32)
        return {'h_t': h_t, 'z': z, 'W': W, 'b': b, 'alpha': alpha}
    _L2_cond_all = _L2_cond_setup()
    _L2_cond_in = {k: v for k, v in _L2_cond_all.items() if k in ('W', 'b', 'alpha')}
    del _L2_cond_all

    def _L3_cond_setup():
        import jax, jax.numpy as jnp
        import numpy as np
        B, T, C = (64, 64, 128)
        key = jax.random.key(seed)
        ks = jax.random.split(key, 17)
        s_in = 1.0 / np.sqrt(C)

        def lin(kw, kb, fan_in):
            s = 1.0 / np.sqrt(fan_in)
            W = jax.random.uniform(kw, (C, fan_in), jnp.float32, -s, s)
            b = jax.random.uniform(kb, (C,), jnp.float32, -s, s)
            return (W, b)
        Wxz, bxz = lin(ks[0], ks[1], C)
        Whz, bhz = lin(ks[2], ks[3], C)
        Wxr, bxr = lin(ks[4], ks[5], C)
        Whr, bhr = lin(ks[6], ks[7], C)
        Wxh, bxh = lin(ks[8], ks[9], C)
        Whh, bhh = lin(ks[10], ks[11], C)
        Whq, bhq = lin(ks[12], ks[13], C)
        X = jax.random.normal(ks[14], (B, T, C), jnp.float32)
        h0 = jax.random.normal(ks[15], (B, C), jnp.float32)
        return {'X': X, 'h0': h0, 'Wxz': Wxz, 'bxz': bxz, 'Whz': Whz, 'bhz': bhz, 'Wxr': Wxr, 'bxr': bxr, 'Whr': Whr, 'bhr': bhr, 'Wxh': Wxh, 'bxh': bxh, 'Whh': Whh, 'bhh': bhh, 'Whq': Whq, 'bhq': bhq}
    _L3_cond_all = _L3_cond_setup()
    _L3_cond_in = {k: v for k, v in _L3_cond_all.items() if k in ('Wxz', 'bxz', 'Whz', 'bhz', 'Wxr', 'bxr', 'Whr', 'bhr', 'Wxh', 'bxh', 'Whh', 'bhh', 'Whq', 'bhq')}
    del _L3_cond_all
    return {'x': x, 'cond_1024': cond_1024, 'L0_cond_weight': _L0_cond_in['weight'], 'L1_cond_conv_b': _L1_cond_in['conv_b'], 'L1_cond_Wp': _L1_cond_in['Wp'], 'L1_cond_bp': _L1_cond_in['bp'], 'L1_cond_Ws': _L1_cond_in['Ws'], 'L1_cond_bs': _L1_cond_in['bs'], 'L1_cond_A_log': _L1_cond_in['A_log'], 'L1_cond_dt_log': _L1_cond_in['dt_log'], 'L1_cond_Wo': _L1_cond_in['Wo'], 'L1_cond_bo': _L1_cond_in['bo'], 'L2_cond_W': _L2_cond_in['W'], 'L2_cond_b': _L2_cond_in['b'], 'L2_cond_alpha': _L2_cond_in['alpha'], 'L3_cond_Wxz': _L3_cond_in['Wxz'], 'L3_cond_bxz': _L3_cond_in['bxz'], 'L3_cond_Whz': _L3_cond_in['Whz'], 'L3_cond_bhz': _L3_cond_in['bhz'], 'L3_cond_Wxr': _L3_cond_in['Wxr'], 'L3_cond_bxr': _L3_cond_in['bxr'], 'L3_cond_Whr': _L3_cond_in['Whr'], 'L3_cond_bhr': _L3_cond_in['bhr'], 'L3_cond_Wxh': _L3_cond_in['Wxh'], 'L3_cond_bxh': _L3_cond_in['bxh'], 'L3_cond_Whh': _L3_cond_in['Whh'], 'L3_cond_bhh': _L3_cond_in['bhh'], 'L3_cond_Whq': _L3_cond_in['Whq'], 'L3_cond_bhq': _L3_cond_in['bhq']}

def reference(x, cond_1024, L0_cond_weight, L1_cond_conv_b, L1_cond_Wp, L1_cond_bp, L1_cond_Ws, L1_cond_bs, L1_cond_A_log, L1_cond_dt_log, L1_cond_Wo, L1_cond_bo, L2_cond_W, L2_cond_b, L2_cond_alpha, L3_cond_Wxz, L3_cond_bxz, L3_cond_Whz, L3_cond_bhz, L3_cond_Wxr, L3_cond_bxr, L3_cond_Whr, L3_cond_bhr, L3_cond_Wxh, L3_cond_bxh, L3_cond_Whh, L3_cond_bhh, L3_cond_Whq, L3_cond_bhq):
    import jax
    import jax.numpy as jnp

    def _L0_cond_ref(Efou, y, weight):
        import jax, jax.numpy as jnp
        import numpy as np
        IN_FEATURES = 128
        OUT_FEATURES = 128
        BATCH = 32
        SEQ = 128
        EPS = 1e-08
        scale = 1.0 / np.sqrt(np.float32(weight.shape[0]))
        ys = y * scale
        d = jax.lax.rsqrt(jnp.einsum('bi,io->bo', ys * ys, weight * weight) + EPS)
        out = jnp.einsum('bsi,io->bso', Efou * ys[:, None, :], weight) * d[:, None, :]
        return out

    def _L1_cond_ref(x, conv_w, conv_b, Wp, bp, Ws, bs, A_log, dt_log, Wo, bo):
        import jax, jax.numpy as jnp
        import numpy as np
        B, L, D = x.shape
        K = conv_w.shape[0]
        N = Ws.shape[1]
        x_pad = jnp.pad(x, ((0, 0), (K - 1, 0), (0, 0)))
        conv = conv_b + sum((x_pad[:, k:k + L, :] * conv_w[k, 0] for k in range(K)))
        proj = conv @ Wp + bp
        B_t = jax.nn.softplus(proj[..., :N])
        C_t = jnp.tanh(proj[..., N:])
        u = x @ Ws + bs
        A = -jax.nn.softplus(A_log)
        dt = jax.nn.softplus(dt_log)
        decay = 1.0 + dt * A

        def step(state, inputs):
            u_t, b_t, c_t = inputs
            state = decay * state + dt * b_t * u_t
            return (state, c_t * state)
        init = jnp.zeros((B, N), dtype=x.dtype)
        xs = tuple((jnp.swapaxes(a, 0, 1) for a in (u, B_t, C_t)))
        _, ys = jax.lax.scan(step, init, xs, unroll=4)
        y = jnp.swapaxes(ys, 0, 1)
        return y @ Wo + bo

    def _L2_cond_ref(h_t, z, W, b, alpha):
        import jax, jax.numpy as jnp
        import numpy as np
        LATENT = 128
        D = h_t.shape[-1]
        Wh = W[:, :D]
        Wz = W[:, D:]
        leak = 1.0 - alpha

        def step(h, z_t):
            gate = jax.nn.sigmoid(h @ Wh.T + z_t @ Wz.T + b)
            h_new = jnp.tanh(h * leak + gate * z_t)
            return (h_new, h_new)
        _, hs = jax.lax.scan(step, h_t, jnp.swapaxes(z, 0, 1))
        return jnp.swapaxes(hs, 0, 1)

    def _L3_cond_ref(X, h0, Wxz, bxz, Whz, bhz, Wxr, bxr, Whr, bhr, Wxh, bxh, Whh, bhh, Whq, bhq):
        import jax, jax.numpy as jnp
        import numpy as np
        B, T, C = (64, 64, 128)
        Xz = jnp.einsum('btc,hc->tbh', X, Wxz) + bxz
        Xr = jnp.einsum('btc,hc->tbh', X, Wxr) + bxr
        Xh = jnp.einsum('btc,hc->tbh', X, Wxh) + bxh

        def step(H, xs):
            xz, xr, xh = xs
            Z = jax.nn.sigmoid(xz + H @ Whz.T + bhz)
            R = jax.nn.sigmoid(xr + H @ Whr.T + bhr)
            H_tilda = jnp.tanh(xh + R * H @ Whh.T + bhh)
            H_new = Z * H + (1.0 - Z) * H_tilda
            Y = H_new @ Whq.T + bhq
            return (H_new, Y)
        _, Ys = jax.lax.scan(step, h0, (Xz, Xr, Xh))
        return jnp.transpose(Ys, (1, 0, 2))
    x = x + _L0_cond_ref(x, cond_1024, L0_cond_weight)
    x = x + _L1_cond_ref(x, cond_1024[:, None, :], L1_cond_conv_b, L1_cond_Wp, L1_cond_bp, L1_cond_Ws, L1_cond_bs, L1_cond_A_log, L1_cond_dt_log, L1_cond_Wo, L1_cond_bo)
    x = x + _L2_cond_ref(cond_1024, x, L2_cond_W, L2_cond_b, L2_cond_alpha)
    x = x + _L3_cond_ref(x, cond_1024, L3_cond_Wxz, L3_cond_bxz, L3_cond_Whz, L3_cond_bhz, L3_cond_Wxr, L3_cond_bxr, L3_cond_Whr, L3_cond_bhr, L3_cond_Wxh, L3_cond_bxh, L3_cond_Whh, L3_cond_bhh, L3_cond_Whq, L3_cond_bhq)
    return x

_drawn_inputs = setup_inputs


def setup_inputs(seed=0):
    import zlib

    import numpy as np

    out = dict(_drawn_inputs(seed))
    spreads = {'L1_cond_conv_b': (0.0, 0.1),
     'L1_cond_bp': (0.0, 0.269),
     'L1_cond_bs': (0.0, 0.1),
     'L1_cond_bo': (0.0, 0.457),
     'L2_cond_alpha': (0.10000000149011612, 0.6)}
    factors = {'L1_cond_A_log': 5.551,
     'L1_cond_dt_log': 3.845,
     'L2_cond_b': 8.0,
     'L3_cond_bxz': 8.0,
     'L3_cond_Whz': 8.0,
     'L3_cond_bhz': 8.0,
     'L3_cond_Wxr': 8.0,
     'L3_cond_bxr': 8.0,
     'L3_cond_Whr': 8.0,
     'L3_cond_bhr': 8.0,
     'L3_cond_bxh': 8.0,
     'L3_cond_Whh': 7.767,
     'L3_cond_bhh': 8.0,
     'L3_cond_bhq': 7.365}
    for name, (base, spread) in spreads.items():
        noise = np.random.default_rng([zlib.crc32(name.encode()), seed]).standard_normal(out[name].shape)
        drawn = base * np.exp(spread * noise) if base else spread * noise
        out[name] = jnp.asarray(drawn.astype(out[name].dtype))
    for name, factor in factors.items():
        out[name] = (out[name] * factor).astype(out[name].dtype)
    return out
```

```python
import concourse.bass as bass
from concourse import mybir
from contextlib import ExitStack

BATCH = 32
TIME = 128
CH = 128
N_STATE = 64
COLS = TIME * BATCH
STEPS = 4
CHUNK = STEPS * BATCH
CHUNKS = TIME // STEPS
BANK = 512
SLABS = COLS // BANK
BLOCK = 32
WINDOWS = TIME // BLOCK
WCOLS = BLOCK * BATCH
GROUPS = CH // BLOCK
ROWLEN = 2 * BLOCK
HALF_B = BATCH // 2
LEAD = 6
EPS = 1e-8

WEIGHTS = ["l0", "wp_b", "wp_c", "wpp_b", "wpp_c", "ws", "wo", "l2_h", "l2_z",
           "hr", "hz", "hh", "xr", "xz", "xh", "hq"]
VECTORS = ["conv_b", "bp_b", "bp_c", "bs", "bo", "a_log", "dt_log", "l2_b", "alpha",
           "bxr", "bhr", "bxz", "bhz", "bxh", "bhh"]


def build(nc, x, cond, weights, vectors, bhq, out):
    f32 = mybir.dt.float32
    ACT = mybir.ActivationFunctionType
    ALU = mybir.AluOpType

    ctx = ExitStack()
    with ctx:
        def sb(name, shape):
            return ctx.enter_context(nc.sbuf_tensor(name, shape, f32))

        def sem(name):
            return ctx.enter_context(nc.semaphore(name))

        x_nat = sb("x_nat", [128, CHUNKS, CH])
        xT = sb("xT", [CH, COLS])
        xs = sb("xs", [CH, COLS])
        x1 = sb("x1", [CH, COLS])
        x1_win = sb("x1_win", [128, BLOCK, WINDOWS, BATCH])
        toep = sb("toep", [128, BLOCK, ROWLEN])
        conv = sb("conv", [CH, COLS])
        soft = sb("soft", [128, TIME * HALF_B + 2])
        log_in = sb("log_in", [128, TIME * HALF_B + 2])
        u_sb = sb("u_sb", [128, TIME * HALF_B])
        gate_c = sb("gate_c", [128, TIME, HALF_B])
        drive = sb("drive", [128, HALF_B, TIME])
        state = sb("state", [128, HALF_B, TIME])
        decay_t = sb("decay_t", [128, HALF_B, TIME])
        gated = sb("gated", [128, TIME, HALF_B])
        x2 = sb("x2", [CH, COLS])
        w_sb = sb("w_sb", [128, len(WEIGHTS), 128])
        v_sb = sb("v_sb", [128, len(VECTORS)])
        bhq_rows = sb("bhq_rows", [128, CH])
        cond_nat = sb("cond_nat", [BATCH, CH])
        condT = sb("condT", [CH, BATCH])
        ysT = sb("ysT", [CH, BATCH])
        ys_sq = sb("ys_sq", [CH, BATCH])
        w0_sq = sb("w0_sq", [CH, CH])
        norm = sb("norm", [CH, 6, BATCH])
        dmod = sb("dmod", [CH, BATCH])
        filt = sb("filt", [CH, ROWLEN])
        filt_end = sb("filt_end", [1, ROWLEN])
        ident = sb("ident", [128, 128])
        flip = sb("flip", [BATCH, BATCH])
        ones = sb("ones", [128, CHUNK])
        proj_b = sb("proj_b", [128, 2])
        dt_a = sb("dt_a", [128, 2])
        leak = sb("leak", [CH, 1])
        gbias = sb("gbias", [CH, 3])
        dbias = sb("dbias", [CH, 4, CH])
        warm = sb("warm", [128, 1])
        half = sb("half", [128, 1])
        halved = sb("halved", [CH, 2, CH])
        r_sb = sb("r_sb", [CH, BATCH])
        z_sb = sb("z_sb", [CH, BATCH])
        q_sb = sb("q_sb", [CH, BATCH])
        zh_sb = sb("zh_sb", [CH, BATCH])
        omz_sb = sb("omz_sb", [CH, BATCH])
        cand_sb = sb("cand_sb", [CH, BATCH])
        new_sb = sb("new_sb", [CH, BATCH])
        hid = sb("hid", [CH, 2, STEPS, BATCH])
        g_sb = sb("g_sb", [CH, BATCH])
        gx_sb = sb("gx_sb", [CH, BATCH])
        s_sb = sb("s_sb", [CH, BATCH])
        h2 = sb("h2", [CH, 2, STEPS, BATCH])
        x3 = sb("x3", [CH, 2, CHUNK])
        y_sb = sb("y_sb", [128, 2, CH])

        filt_dram = nc.dram_tensor("filt_dram", [(CH + 1) * ROWLEN], f32, kind="Internal")

        ps = ctx.enter_context(nc.psum_tensor("ps", [128, 8, BANK], f32))
        ps_r = [ps[:, 0, 0:CHUNK], ps[:, 1, 0:CHUNK]]
        ps_z = [ps[:, 2, 0:CHUNK], ps[:, 3, 0:CHUNK]]
        ps_c = [ps[:, 4, 0:CHUNK], ps[:, 5, 0:CHUNK]]
        ps_g = ps[:, 6, 0:CHUNK]
        ps_y = ps[:, 7, 0:CHUNK]
        SMALL = 7

        def w(name):
            return w_sb[:, WEIGHTS.index(name), :]

        def vec(name):
            k = VECTORS.index(name)
            return v_sb[:, k:k + 1]

        dt = soft[:, TIME * HALF_B + 1:TIME * HALF_B + 2]
        SOFT_AD = slice(TIME * HALF_B, TIME * HALF_B + 2)

        def soft_cols(j):
            return slice(j * BANK, (j + 1) * BANK)

        def bcast(t, n):
            return t[:, :].rearrange("p (o b) -> p o b", o=1).to_broadcast([CH, n, BATCH])

        def tb(t, lo, n):
            return t[:, lo:lo + n].rearrange("p (t b) -> p t b", b=BATCH)

        ld_cond, ld_w0, ld_w, ld_v, ld_bhq = (
            sem(n) for n in ("ld_cond", "ld_w0", "ld_w", "ld_v", "ld_bhq"))
        ld_x = [sem("ld_x_first_half"), sem("ld_x_second_half")]
        st_filt, ld_toep = sem("st_filt"), sem("ld_toep")
        const_ready = sem("const_ready")
        cond_turned = sem("cond_turned")
        filt_done = sem("filt_done")
        ys_done, sq_done = sem("ys_done"), sem("sq_done")
        norm_mm, norm_in, norm_root, norm_step = (
            sem(n) for n in ("norm_mm", "norm_in", "norm_root", "norm_step"))
        x_turned, xT_done, xs_done, l0_mm, l0_scaled, x1_done = (
            sem(n) for n in ("x_turned", "xT_done", "xs_done", "l0_mm", "l0_scaled", "x1_done"))
        win_done, conv_mm, conv_done = sem("win_done"), sem("conv_mm"), sem("conv_done")
        pb_mm, pb_done = sem("pb_mm"), sem("pb_done")
        relu_done, abs_done, tanh_done, log_done, soft_done = (
            sem(n) for n in ("relu_done", "abs_done", "tanh_done", "log_done", "soft_done"))
        decay_step = sem("decay_step")
        u_mm, b_mm, c_mm, u_done = sem("u_mm"), sem("b_mm"), sem("c_mm"), sem("u_done")
        c_done = sem("c_done")
        drive_done, scan_done, gated_done, y_mm, x2_done = (
            sem(n) for n in ("drive_done", "scan_done", "gated_done", "y_mm", "x2_done"))
        vec_done = sem("vec_done")
        pre_g, pre_sig, pre_gx, pre_s, pre_h = (
            sem(n) for n in ("pre_g", "pre_sig", "pre_gx", "pre_s", "pre_h"))
        r_ready, z_ready, c_ready, g_ready = (
            sem(n) for n in ("r_ready", "z_ready", "c_ready", "g_ready"))
        r_sig, z_sig, c_tanh, g_sig, h2_done = (
            sem(n) for n in ("r_sig", "z_sig", "c_tanh", "g_sig", "h2_done"))
        q_done, zh_done, omz_done, new_done, hid_done, gx_done, s_done = (
            sem(n) for n in ("q_done", "zh_done", "omz_done", "new_done", "hid_done", "gx_done",
                             "s_done"))
        x3_done, y_ready, y_done = sem("x3_done"), sem("y_ready"), sem("y_done")
        out_sent = [sem("out_sent_even"), sem("out_sent_odd")]

        out_v = out.rearrange("b (c s) d -> c s b d", s=STEPS)

        block = ctx.enter_context(nc.Block())

        @block.sync
        def _(sp_eng):
            sp_eng.dma_start(cond_nat[:, :], cond).then_inc(ld_cond, 16)
            x_v = x.rearrange("b (c s) d -> s b c d", s=STEPS)
            hc = CHUNKS // 2
            for half in range(2):
                for s in range(STEPS):
                    sp_eng.dma_start(x_nat[s * BATCH:(s + 1) * BATCH, half * hc:(half + 1) * hc, :],
                                     x_v[s, :, half * hc:(half + 1) * hc, :]).then_inc(ld_x[half], 16)
            sp_eng.wait_ge(filt_done, 2)
            sp_eng.dma_start(filt_dram[0:CH * ROWLEN].rearrange("(d m) -> d m", m=ROWLEN),
                             filt[:, :]).then_inc(st_filt, 16)
            sp_eng.dma_start(filt_dram[CH * ROWLEN:(CH + 1) * ROWLEN].rearrange("(o m) -> o m", o=1),
                             filt_end[:, :]).then_inc(st_filt, 16)
            sp_eng.wait_ge(st_filt, 32)
            for g in range(GROUPS):
                src = bass.AP(filt_dram, g * BLOCK * ROWLEN, [[1, BLOCK], [1, BLOCK * ROWLEN]])
                sp_eng.dma_start(toep[g * BLOCK:(g + 1) * BLOCK, :, :]
                                 .rearrange("p d m -> p (d m)"), src).then_inc(ld_toep, 16)
            sp_eng.dma_start(w_sb[:, 1:, :], weights[:, 1:, :]).then_inc(ld_w, 16)
            sp_eng.dma_start(bhq_rows[:, :], bhq.rearrange("(o n) -> o n", o=1)
                             .to_broadcast([128, CH])).then_inc(ld_bhq, 16)

            def send(pair, par, c):
                sp_eng.wait_ge(y_done, c + 1)
                sp_eng.dma_start(out_v[bass.ds(c, 1), :, :, :].rearrange("o s b d -> (o s) b d"),
                                 y_sb[:, par, :]).then_inc(out_sent[par], 16)

            with sp_eng.Fori(0, CHUNKS // 2) as pair:
                send(pair, 0, pair * 2)
                send(pair, 1, pair * 2 + 1)
            for par in range(2):
                sp_eng.wait_ge(out_sent[par], 16 * (CHUNKS // 2 + par))

        @block.gpsimd
        def _(pool):
            nc.gpsimd.memset(ident[:, :], 0.0).then_inc(const_ready, 1)
            nc.gpsimd.memset(flip[:, :], 0.0).then_inc(const_ready, 1)
            pool.wait_ge(const_ready, 2)
            nc.gpsimd.affine_select(out=ident[:, :], in_=ident[:, :], compare_op=ALU.not_equal,
                                    fill=1.0, base=0, pattern=[[-1, 128]],
                                    channel_multiplier=1).then_inc(const_ready, 1)
            nc.gpsimd.affine_select(out=flip[:, :], in_=flip[:, :], compare_op=ALU.not_equal,
                                    fill=1.0, base=1 - BATCH, pattern=[[1, BATCH]],
                                    channel_multiplier=1).then_inc(const_ready, 1)
            nc.gpsimd.memset(filt[:, :], 0.0).then_inc(const_ready, 1)
            nc.gpsimd.memset(filt_end[:, :], 0.0).then_inc(const_ready, 1)
            nc.gpsimd.memset(ones[:, :], 1.0).then_inc(const_ready, 1)
            nc.gpsimd.memset(half[:, :], 0.5).then_inc(const_ready, 1)
            nc.gpsimd.memset(decay_t[:, :, :], 1.0).then_inc(const_ready, 1)
            pool.wait_ge(const_ready, 9)
            nc.gpsimd.memset(decay_t[:, :, 0:1], 0.0).then_inc(const_ready, 1)

        @block.scalar
        def _(act):
            act.dma_start(w_sb[:, 0, :], weights[:, 0, :]).then_inc(ld_w0, 16)
            act.dma_start(v_sb[:, :], vectors).then_inc(ld_v, 16)
            act.wait_ge(norm_in, 1)
            nc.scalar.activation(norm[:, 1, :], norm[:, 0, :], ACT.Sqrt).then_inc(norm_root, 1)
            for q in range(SLABS):
                act.wait_ge(x_turned, q + 1)
                nc.scalar.activation(xT[:, q * BANK:(q + 1) * BANK], ps[:, q % 2, :],
                                     ACT.Copy).then_inc(xT_done, 1)
            def soft_start(cols, v, bias, count):
                nc.scalar.activation(soft[:, cols], v, ACT.Relu, bias=bias).then_inc(relu_done, 1)
                nc.scalar.activation(log_in[:, cols], v, ACT.Abs, bias=bias).then_inc(abs_done, 1)
                act.wait_ge(abs_done, count)
                nc.scalar.activation(log_in[:, cols], log_in[:, cols], ACT.Tanh,
                                     scale=0.5).then_inc(tanh_done, 1)

            act.wait_ge(ld_v, 16)
            k = VECTORS.index("a_log")
            soft_start(SOFT_AD, v_sb[:, k:k + 2], 0.0, 1)
            act.wait_ge(pb_done, 2)
            for j in range(WINDOWS):
                base = 4 * (j % 2)
                act.wait_ge(b_mm, j + 1)
                soft_start(soft_cols(j), ps[:, base + 1, :], proj_b[:, 0:1], j + 2)
                act.wait_ge(c_mm, j + 1)
                nc.scalar.activation(gate_c[:, j * BLOCK:(j + 1) * BLOCK, :], ps[:, base + 2, :]
                                     .rearrange("p (t b) -> p t b", b=HALF_B), ACT.Tanh,
                                     bias=proj_b[:, 1:2]).then_inc(c_done, 1)
            act.wait_ge(tanh_done, WINDOWS + 1)
            for cols in [SOFT_AD] + [soft_cols(j) for j in range(WINDOWS)]:
                nc.scalar.activation(log_in[:, cols], log_in[:, cols], ACT.Ln,
                                     scale=0.5, bias=half[:, 0:1]).then_inc(log_done, 1)
            nc.scalar.activation(warm[:, :], ones[:, 0:1], ACT.Tanh)

            for t in range(LEAD):
                act.wait_ge(pre_g, t + 1)
                nc.scalar.activation(g_sb[:, :], ps_g[:, (t % STEPS) * BATCH:(t % STEPS + 1) * BATCH],
                                     ACT.Tanh, scale=0.5).then_inc(pre_sig, 1)
                act.wait_ge(pre_s, t + 1)
                nc.scalar.activation(h2[:, t // STEPS % 2, t % STEPS, :], s_sb[:, :],
                                     ACT.Tanh, scale=0.5).then_inc(pre_h, 1)

            def step(n, k8, l2):
                par, k = k8 // STEPS, k8 % STEPS
                here = slice(k * BATCH, (k + 1) * BATCH)
                par2, k2 = (k8 + LEAD) // STEPS % 2, (k8 + LEAD) % STEPS
                act.wait_ge(r_ready, n)
                nc.scalar.activation(r_sb[:, :], ps_r[par][:, here], ACT.Tanh,
                                     scale=0.5).then_inc(r_sig, 1)
                act.wait_ge(z_ready, n)
                nc.scalar.activation(z_sb[:, :], ps_z[par][:, here], ACT.Tanh,
                                     scale=0.5).then_inc(z_sig, 1)
                if l2:
                    act.wait_ge(g_ready, n)
                    nc.scalar.activation(g_sb[:, :], ps_g[:, k2 * BATCH:(k2 + 1) * BATCH],
                                         ACT.Tanh, scale=0.5).then_inc(g_sig, 1)
                act.wait_ge(c_ready, n)
                nc.scalar.activation(cand_sb[:, :], ps_c[par][:, here], ACT.Tanh).then_inc(c_tanh, 1)
                if l2:
                    act.wait_ge(s_done, n)
                    nc.scalar.activation(h2[:, par2, k2, :], s_sb[:, :], ACT.Tanh,
                                         scale=0.5).then_inc(h2_done, 1)

            pairs = CHUNKS // 2
            with act.Fori(0, pairs - 1) as pair:
                for k8 in range(2 * STEPS):
                    step(pair * (2 * STEPS) + (k8 + 1), k8, True)
            for k8 in range(2 * STEPS):
                step((pairs - 1) * 2 * STEPS + k8 + 1, k8, k8 < 2 * STEPS - LEAD)

        @block.vector
        def _(dve):
            dve.wait_ge(cond_turned, 2)
            dve.wait_ge(const_ready, 6)
            nc.vector.tensor_copy(filt[:, BLOCK - 1:2 * BLOCK - 1],
                                  ps[:, SMALL, BATCH:2 * BATCH]).then_inc(filt_done, 2)
            nc.vector.tensor_copy(condT[:, :], ps[:, SMALL, 0:BATCH]).then_inc(ys_done, 1)
            nc.vector.tensor_scalar(ysT[:, :], ps[:, SMALL, 0:BATCH], float(CH) ** -0.5, None,
                                    ALU.mult).then_inc(ys_done, 1)
            dve.wait_ge(ys_done, 2)
            nc.vector.tensor_tensor(ys_sq[:, :], ysT[:, :], ysT[:, :], ALU.mult).then_inc(sq_done, 1)
            dve.wait_ge(ld_w0, 16)
            nc.vector.tensor_tensor(w0_sq[:, :], w("l0"), w("l0"), ALU.mult).then_inc(sq_done, 1)
            dve.wait_ge(norm_mm, 1)
            nc.vector.tensor_scalar(norm[:, 0, :], ps[:, SMALL, 2 * BATCH:3 * BATCH], EPS, None,
                                    ALU.add).then_inc(norm_in, 1)
            dve.wait_ge(norm_root, 1)
            nc.vector.reciprocal(norm[:, 2, :], norm[:, 1, :]).then_inc(norm_step, 1)
            dve.wait_ge(norm_step, 1)
            nc.vector.tensor_tensor(norm[:, 3, :], norm[:, 2, :], norm[:, 2, :],
                                    ALU.mult).then_inc(norm_step, 1)
            dve.wait_ge(norm_step, 2)
            nc.vector.tensor_tensor(norm[:, 4, :], norm[:, 3, :], norm[:, 0, :],
                                    ALU.mult).then_inc(norm_step, 1)
            dve.wait_ge(norm_step, 3)
            nc.vector.tensor_scalar(norm[:, 5, :], norm[:, 4, :], -0.5, 1.5, ALU.mult,
                                    ALU.add).then_inc(norm_step, 1)
            dve.wait_ge(norm_step, 4)
            nc.vector.tensor_tensor(dmod[:, :], norm[:, 2, :], norm[:, 5, :],
                                    ALU.mult).then_inc(norm_step, 1)
            dve.wait_ge(norm_step, 5)

            slab_t = BANK // BATCH

            def finish_x1(q):
                lo = q * BANK
                dve.wait_ge(l0_mm, q + 1)
                nc.vector.tensor_tensor(tb(x1, lo, BANK), ps[:, 2 + q % 2, :]
                                        .rearrange("p (t b) -> p t b", b=BATCH),
                                        bcast(dmod, slab_t), ALU.mult).then_inc(l0_scaled, 1)
                dve.wait_ge(l0_scaled, q + 1)
                nc.vector.tensor_tensor(x1[:, lo:lo + BANK], x1[:, lo:lo + BANK],
                                        xT[:, lo:lo + BANK], ALU.add).then_inc(x1_done, 1)

            for q in range(SLABS):
                lo = q * BANK
                dve.wait_ge(xT_done, q + 1)
                nc.vector.tensor_tensor(tb(xs, lo, BANK), tb(xT, lo, BANK), bcast(ysT, slab_t),
                                        ALU.mult).then_inc(xs_done, 1)
                if q > 0:
                    finish_x1(q - 1)
            finish_x1(SLABS - 1)
            for j in range(WINDOWS):
                dve.wait_ge(x1_done, (j + 1) * SLABS // WINDOWS)
                nc.vector.transpose(
                    x1_win[:, :, j, :].rearrange("p d b -> p b d"),
                    tb(x1, j * WCOLS, WCOLS)[:, ::-1, :].rearrange("p t b -> p b t")
                ).then_inc(win_done, 1)
            dve.wait_ge(ld_v, 16)
            dve.wait_ge(const_ready, 10)
            nc.vector.tensor_scalar(leak[:, :], vec("alpha"), -2.0, 2.0, ALU.mult,
                                    ALU.add).then_inc(vec_done, 1)
            for k, gate in enumerate(("r", "z", "h")):
                nc.vector.tensor_tensor(gbias[:, k:k + 1], vec("bx" + gate), vec("bh" + gate),
                                        ALU.add).then_inc(vec_done, 1)
            dve.wait_ge(vec_done, 4)
            for k in range(3):
                nc.vector.tensor_scalar(dbias[:, k, :], ident[:, :], gbias[:, k:k + 1], None,
                                        ALU.mult).then_inc(vec_done, 1)
            nc.vector.tensor_scalar(dbias[:, 3, :], ident[:, :], vec("l2_b"), None,
                                    ALU.mult).then_inc(vec_done, 1)
            dve.wait_ge(ld_w, 16)
            for k, name in enumerate(("hr", "hh")):
                nc.vector.tensor_scalar(halved[:, k, :], w(name), 0.5, None,
                                        ALU.mult).then_inc(vec_done, 1)
            dve.wait_ge(pb_mm, 2)
            nc.vector.tensor_tensor(proj_b[:, 0:1], ps[:, SMALL, 96:97], vec("bp_b"),
                                    ALU.add).then_inc(pb_done, 1)
            nc.vector.tensor_tensor(proj_b[:, 1:2], ps[:, SMALL, 97:98], vec("bp_c"),
                                    ALU.add).then_inc(pb_done, 1)
            for h in range(2):
                dve.wait_ge(conv_mm, h + 1)
                src = ps[:, 4 * h:4 * h + 4, :].rearrange("p a (m jj b) -> p jj b (a m)", jj=2, b=BATCH)
                for jj in range(2):
                    nc.vector.transpose(
                        tb(conv, (2 * h + jj) * WCOLS, WCOLS).rearrange("p t b -> p b t"),
                        src[:, jj, :, :]).then_inc(conv_done, 1)
            for j in range(WINDOWS):
                dve.wait_ge(u_mm, j + 1)
                nc.vector.tensor_copy(u_sb[:, soft_cols(j)], ps[:, 4 * (j % 2), :]).then_inc(u_done, 1)
            dve.wait_ge(log_done, 1)
            nc.vector.tensor_tensor(soft[:, SOFT_AD], soft[:, SOFT_AD], log_in[:, SOFT_AD],
                                    ALU.subtract).then_inc(soft_done, 1)
            dve.wait_ge(soft_done, 1)
            nc.vector.tensor_tensor(dt_a[:, 0:1], soft[:, SOFT_AD.start:SOFT_AD.start + 1], dt,
                                    ALU.mult).then_inc(decay_step, 1)
            dve.wait_ge(decay_step, 1)
            nc.vector.tensor_scalar(dt_a[:, 1:2], dt_a[:, 0:1], -1.0, 1.0, ALU.mult,
                                    ALU.add).then_inc(decay_step, 1)
            dve.wait_ge(decay_step, 2)
            nc.vector.tensor_scalar(decay_t[:, :, :], decay_t[:, :, :], dt_a[:, 1:2], None,
                                    ALU.mult).then_inc(decay_step, 1)
            for j in range(WINDOWS):
                dve.wait_ge(log_done, j + 2)
                nc.vector.tensor_tensor(soft[:, soft_cols(j)], soft[:, soft_cols(j)],
                                        log_in[:, soft_cols(j)], ALU.subtract).then_inc(soft_done, 1)
                dve.wait_ge(soft_done, j + 2)
                nc.vector.scalar_tensor_tensor(
                    out=drive[:, :, j * BLOCK:(j + 1) * BLOCK].rearrange("p b t -> p t b"),
                    in0=u_sb[:, soft_cols(j)].rearrange("p (t b) -> p t b", b=HALF_B),
                    scalar=vec("bs"),
                    in1=soft[:, soft_cols(j)].rearrange("p (t b) -> p t b", b=HALF_B),
                    op0=ALU.add, op1=ALU.mult).then_inc(drive_done, 1)
            dve.wait_ge(drive_done, WINDOWS)
            dve.wait_ge(decay_step, 3)
            nc.vector.tensor_tensor_scan(state[:, :, :].rearrange("p b t -> p (b t)"),
                                         decay_t[:, :, :].rearrange("p b t -> p (b t)"),
                                         drive[:, :, :].rearrange("p b t -> p (b t)"),
                                         0.0, ALU.mult, ALU.add).then_inc(scan_done, 1)
            dve.wait_ge(scan_done, 1)
            dve.wait_ge(c_done, WINDOWS)
            for j in range(WINDOWS):
                ts = slice(j * BLOCK, (j + 1) * BLOCK)
                nc.vector.scalar_tensor_tensor(
                    out=gated[:, ts, :], in0=state[:, :, ts].rearrange("p b t -> p t b"),
                    scalar=dt, in1=gate_c[:, ts, :], op0=ALU.mult, op1=ALU.mult
                ).then_inc(gated_done, 1)
            for j in range(WINDOWS):
                dve.wait_ge(y_mm, 2 * (j + 1))
                for hb in range(2):
                    cols = slice(hb * HALF_B, (hb + 1) * HALF_B)
                    nc.vector.scalar_tensor_tensor(
                        out=tb(x2, j * WCOLS, WCOLS)[:, :, cols],
                        in0=ps[:, 2 + hb + 4 * (j % 2), :].rearrange("p (t b) -> p t b", b=HALF_B),
                        scalar=vec("bo"), in1=tb(x1, j * WCOLS, WCOLS)[:, :, cols],
                        op0=ALU.add, op1=ALU.add).then_inc(x2_done, 1)
            dve.wait_ge(ys_done, 2)
            nc.vector.tensor_copy(h2[:, 1, STEPS - 1, :], condT[:, :]).then_inc(pre_h, 1)
            nc.vector.tensor_copy(hid[:, 1, STEPS - 1, :], condT[:, :]).then_inc(hid_done, 1)
            dve.wait_ge(pre_h, 1)
            dve.wait_ge(x2_done, 2 * WINDOWS)
            for t in range(LEAD):
                dve.wait_ge(pre_sig, t + 1)
                nc.vector.scalar_tensor_tensor(
                    out=gx_sb[:, :], in0=g_sb[:, :], scalar=1.0, in1=x2[:, t * BATCH:(t + 1) * BATCH],
                    op0=ALU.add, op1=ALU.mult).then_inc(pre_gx, 1)
                dve.wait_ge(pre_gx, t + 1)
                nc.vector.scalar_tensor_tensor(
                    out=s_sb[:, :], in0=h2[:, (t - 1) // STEPS % 2, (t - 1) % STEPS, :],
                    scalar=leak[:, :], in1=gx_sb[:, :], op0=ALU.mult, op1=ALU.add
                ).then_inc(pre_s, 1)
                if t % STEPS == STEPS - 1:
                    c = t // STEPS
                    dve.wait_ge(pre_h, t + 2)
                    nc.vector.tensor_tensor(x3[:, c % 2, :], x2[:, c * CHUNK:(c + 1) * CHUNK],
                                            h2[:, c % 2, :, :].rearrange("p s b -> p (s b)"),
                                            ALU.add).then_inc(x3_done, 1)
            dve.wait_ge(ld_bhq, 16)
            nc.vector.memset(y_sb[:, 1, :], 0.0).then_inc(out_sent[1], 16)

            def send_y(c, par, sent):
                if not isinstance(sent, int) or sent > 0:
                    dve.wait_ge(out_sent[par], sent)
                dve.wait_ge(y_ready, c + 1)
                nc.vector.tensor_tensor(y_sb[:, par, :], ps_y, bhq_rows[:, :],
                                        ALU.add).then_inc(y_done, 1)

            def step(n, t_off, k8, l2, out_chunk, out_count):
                par, k = k8 // STEPS, k8 % STEPS
                prev = hid[:, (k8 - 1) // STEPS % 2, (k8 - 1) % STEPS, :]
                t2 = k8 + LEAD
                par2, k2 = t2 // STEPS % 2, t2 % STEPS
                prev2 = h2[:, (t2 - 1) // STEPS % 2, (t2 - 1) % STEPS, :]
                dve.wait_ge(r_sig, n)
                dve.wait_ge(hid_done, n)
                nc.vector.scalar_tensor_tensor(out=q_sb[:, :], in0=r_sb[:, :], scalar=1.0, in1=prev,
                                               op0=ALU.add, op1=ALU.mult).then_inc(q_done, 1)
                dve.wait_ge(z_sig, n)
                nc.vector.scalar_tensor_tensor(out=zh_sb[:, :], in0=z_sb[:, :], scalar=1.0, in1=prev,
                                               op0=ALU.add, op1=ALU.mult).then_inc(zh_done, 1)
                nc.vector.tensor_scalar(omz_sb[:, :], z_sb[:, :], -0.5, 0.5, ALU.mult,
                                        ALU.add).then_inc(omz_done, 1)
                if l2:
                    dve.wait_ge(g_sig, n)
                    col = t_off + (k8 + LEAD) * BATCH
                    nc.vector.scalar_tensor_tensor(
                        out=gx_sb[:, :], in0=g_sb[:, :], scalar=1.0, in1=x2[:, bass.ds(col, BATCH)],
                        op0=ALU.add, op1=ALU.mult).then_inc(gx_done, 1)
                    dve.wait_ge(gx_done, n)
                    nc.vector.scalar_tensor_tensor(out=s_sb[:, :], in0=prev2, scalar=leak[:, :],
                                                   in1=gx_sb[:, :], op0=ALU.mult,
                                                   op1=ALU.add).then_inc(s_done, 1)
                dve.wait_ge(c_tanh, n)
                dve.wait_ge(omz_done, n)
                nc.vector.tensor_tensor(new_sb[:, :], omz_sb[:, :], cand_sb[:, :],
                                        ALU.mult).then_inc(new_done, 1)
                dve.wait_ge(new_done, n)
                nc.vector.scalar_tensor_tensor(out=hid[:, par, k, :], in0=zh_sb[:, :], scalar=0.5,
                                               in1=new_sb[:, :], op0=ALU.mult,
                                               op1=ALU.add).then_inc(hid_done, 1)
                if k == 1 and out_count is not None:
                    send_y(out_chunk, 1 - par, out_count)
                if l2 and k2 == STEPS - 1:
                    dve.wait_ge(h2_done, n)
                    lo = t_off + (k8 + LEAD - (STEPS - 1)) * BATCH
                    nc.vector.tensor_tensor(x3[:, par2, :], x2[:, bass.ds(lo, CHUNK)],
                                            h2[:, par2, :, :].rearrange("p s b -> p (s b)"),
                                            ALU.add).then_inc(x3_done, 1)

            pairs = CHUNKS // 2

            def chunk_pair(pair, peeled, last):
                for k8 in range(2 * STEPS):
                    par = k8 // STEPS
                    out_chunk = pair * 2 + (par - 1)
                    out_count = None if peeled and par == 0 else pair * 16
                    step(pair * (2 * STEPS) + (k8 + 1), pair * (2 * CHUNK), k8,
                         not last or k8 < 2 * STEPS - LEAD, out_chunk, out_count)

            chunk_pair(0, True, False)
            with dve.Fori(1, pairs - 1) as pair:
                chunk_pair(pair, False, False)
            chunk_pair(pairs - 1, False, True)
            send_y(CHUNKS - 1, 1, 16 * pairs)

        @block.tensor
        def _(pe):
            def mm(o, lhsT, rhs, start=True, stop=True):
                return nc.tensor.matmul(o, lhsT, rhs, start=start, stop=stop, skip_group_check=True)

            pe.wait_ge(const_ready, 4)
            pe.wait_ge(ld_cond, 16)
            nc.tensor.transpose(ps[:, SMALL, 0:BATCH], cond_nat[:, :],
                                ident[0:BATCH, 0:BATCH]).then_inc(cond_turned, 1)
            nc.tensor.transpose(ps[:, SMALL, BATCH:2 * BATCH], cond_nat[:, :],
                                flip[:, :]).then_inc(cond_turned, 1)
            pe.wait_ge(ys_done, 2)
            pe.wait_ge(sq_done, 2)
            mm(ps[:, SMALL, 2 * BATCH:3 * BATCH], w0_sq[:, :], ys_sq[:, :]).then_inc(norm_mm, 1)

            per = BANK // CHUNK

            def turn_x(q):
                if q == 0:
                    pe.wait_ge(ld_x[0], 16 * STEPS)
                if q == SLABS // 2:
                    pe.wait_ge(ld_x[1], 16 * STEPS)
                if q >= 2:
                    pe.wait_ge(xT_done, q - 1)
                for i in range(per):
                    last = nc.tensor.transpose(ps[:, q % 2, i * CHUNK:(i + 1) * CHUNK],
                                               x_nat[:, q * per + i, :], ident[:, :])
                last.then_inc(x_turned, 1)

            turn_x(0)
            for q in range(SLABS):
                if q + 1 < SLABS:
                    turn_x(q + 1)
                pe.wait_ge(xs_done, q + 1)
                if q >= 2:
                    pe.wait_ge(l0_scaled, q - 1)
                mm(ps[:, 2 + q % 2, :], w("l0"), xs[:, q * BANK:(q + 1) * BANK]).then_inc(l0_mm, 1)

            pe.wait_ge(ld_v, 16)
            pe.wait_ge(ld_w, 16)
            for k, name in enumerate(("wp_b", "wp_c")):
                mm(ps[:, SMALL, 96 + k:97 + k], w(name), vec("conv_b")).then_inc(pb_mm, 1)

            pe.wait_ge(ld_toep, 16 * GROUPS)
            for h in range(2):
                if h == 0:
                    pe.wait_ge(xT_done, SLABS)
                    pe.wait_ge(l0_scaled, SLABS)
                else:
                    pe.wait_ge(pb_done, 2)
                    pe.wait_ge(norm_in, 1)
                pe.wait_ge(win_done, 2 * (h + 1))
                for i in range(BLOCK):
                    for prev in range(2):
                        for g in range(GROUPS):
                            rows = slice(g * BLOCK, (g + 1) * BLOCK)
                            place = (i + g * (BLOCK // GROUPS)) % BLOCK
                            bank, at = 4 * h + place // 8, place % 8 * 2 * BATCH
                            if not prev:
                                j0, cols = 2 * h, 2 * BATCH
                            elif h == 0:
                                j0, cols, at = 0, BATCH, at + BATCH
                            else:
                                j0, cols = 2 * h - 1, 2 * BATCH
                            rhs = x1_win[rows, i, :, :].rearrange("p j b -> p (j b)")
                            last = mm(ps[rows, bank, at:at + cols],
                                      toep[rows, i, prev * BLOCK:(prev + 1) * BLOCK],
                                      rhs[:, j0 * BATCH:j0 * BATCH + cols],
                                      start=not prev, stop=bool(prev))
                last.then_inc(conv_mm, 1)

            for j in range(WINDOWS):
                base = 4 * (j % 2)
                if j < 2:
                    pe.wait_ge(conv_done, 2 * (j + 1))
                else:
                    pe.wait_ge(u_done, j - 1)
                    pe.wait_ge(c_done, j - 1)
                if j == 0:
                    pe.wait_ge(conv_done, 2)
                for k, (name, src, done) in enumerate((("ws", x1, u_mm), ("wpp_b", conv, b_mm),
                                                       ("wpp_c", conv, c_mm))):
                    for hb in range(2):
                        rhs = tb(src, j * WCOLS, WCOLS)[:, :, hb * HALF_B:(hb + 1) * HALF_B]
                        last = mm(ps[hb * N_STATE:(hb + 1) * N_STATE, base + k, :],
                                  w(name)[:, 0:N_STATE], rhs)
                    last.then_inc(done, 1)
            for j in range(WINDOWS):
                if j == 0:
                    pe.wait_ge(c_done, WINDOWS)
                    pe.wait_ge(gated_done, WINDOWS)
                if j >= 2:
                    pe.wait_ge(x2_done, 2 * (j - 1))
                for hb in range(2):
                    rows = slice(hb * N_STATE, (hb + 1) * N_STATE)
                    mm(ps[:, 2 + hb + 4 * (j % 2), :], w("wo")[rows, :],
                       gated[rows, j * BLOCK:(j + 1) * BLOCK, :].rearrange("p t b -> p (t b)")
                       ).then_inc(y_mm, 1)

            DIAG = {"r": 0, "z": 1, "h": 2, "g": 3}

            def bias(o, gate):
                return mm(o, dbias[:, DIAG[gate], :], ones[:, :], stop=False)

            def project(o, name, rhs):
                return mm(o, w(name), rhs, start=False)

            def project_twice(o, name, rhs):
                return mm(o, halved[:, ("hr", "hh").index(name), :], rhs, start=False)

            def keep_streaming(o):
                return mm(o, ident[:, :], ones[:, :])

            def at_step(o, k):
                return o[:, k * BATCH:(k + 1) * BATCH]

            pe.wait_ge(vec_done, 10)
            pe.wait_ge(x2_done, 2 * WINDOWS)
            for t in range(LEAD):
                if t % STEPS == 0:
                    if t:
                        pe.wait_ge(pre_sig, t)
                    bias(ps_g, "g")
                    project(ps_g, "l2_z", x2[:, t * BATCH:t * BATCH + CHUNK])
                pe.wait_ge(pre_h, t + 1)
                project(at_step(ps_g, t % STEPS), "l2_h",
                        h2[:, (t - 1) // STEPS % 2, (t - 1) % STEPS, :]).then_inc(pre_g, 1)
                for _ in range(2):
                    mm(ps[:, 7, :], w("l2_z"), x2[:, 0:BANK])
                if t == STEPS:
                    pe.wait_ge(x3_done, 1)
                    for gate, o in (("r", ps_r), ("z", ps_z), ("h", ps_c)):
                        bias(o[0], gate)
                        project(o[0], "x" + gate, x3[:, 0, :])

            pe.wait_ge(hid_done, 1)
            h_init = hid[:, 1, STEPS - 1, :]
            project(at_step(ps_r[0], 0), "hr", h_init).then_inc(r_ready, 1)
            project(at_step(ps_z[0], 0), "hz", h_init).then_inc(z_ready, 1)
            pe.wait_ge(pre_h, LEAD + 1)
            project(at_step(ps_g, LEAD % STEPS), "l2_h",
                    h2[:, (LEAD - 1) // STEPS % 2, (LEAD - 1) % STEPS, :]).then_inc(g_ready, 1)

            def fill(slot, pair, par, first, last_chunk, no_l2):
                nxt = 1 - par
                if slot == 1 and not first:
                    mm(ps_y, x3[:, nxt, :], ident[:, :], start=False).then_inc(y_ready, 1)
                elif slot > 9 or last_chunk or slot == 1 or (slot in (4, 5) and no_l2):
                    if slot > 9 and not last_chunk:
                        if not first:
                            pe.wait_ge(y_done, pair * 2 + par)
                        keep_streaming(ps_y)
                    else:
                        keep_streaming(ps_c[nxt])
                if last_chunk:
                    return
                if slot == 2:
                    bias(ps_r[nxt], "r")
                if slot == 3:
                    bias(ps_z[nxt], "z")
                if slot == 4 and not no_l2:
                    pe.wait_ge(g_sig, pair * (2 * STEPS) + (par * STEPS + 2))
                    bias(ps_g, "g")
                if slot == 5 and not no_l2:
                    lo = pair * (2 * CHUNK) + (par + 2) * CHUNK
                    project(ps_g, "l2_z", x2[:, bass.ds(lo, CHUNK)])
                if slot == 6:
                    bias(ps_c[nxt], "h")
                if slot == 7:
                    pe.wait_ge(x3_done, pair * 2 + (par + 2))
                    project(ps_r[nxt], "xr", x3[:, nxt, :])
                if slot == 8:
                    project(ps_z[nxt], "xz", x3[:, nxt, :])
                if slot == 9:
                    project(ps_c[nxt], "xh", x3[:, nxt, :])

            def step(pair, k8, peeled, last):
                par, k = k8 // STEPS, k8 % STEPS
                n = pair * (2 * STEPS) + (k8 + 1)
                first = peeled and par == 0
                last_chunk = last and par == 1
                no_l2 = last
                nxt8 = (k8 + 1) % (2 * STEPS)
                npar, nk = nxt8 // STEPS, nxt8 % STEPS
                if last and k8 == 2 * STEPS - 1:
                    pe.wait_ge(q_done, n)
                    project_twice(at_step(ps_c[par], k), "hh", q_sb[:, :]).then_inc(c_ready, 1)
                    return
                pe.wait_ge(q_done, n)
                project_twice(at_step(ps_c[par], k), "hh", q_sb[:, :]).then_inc(c_ready, 1)
                for slot in {0: (1, 2), 1: (4, 5), 2: (7, 8), 3: (9, 10)}[k]:
                    fill(slot, pair, par, first, last_chunk, no_l2)
                pe.wait_ge(zh_done, n)
                project_twice(at_step(ps_r[npar], nk), "hr", zh_sb[:, :])
                pe.wait_ge(new_done, n)
                project(at_step(ps_r[npar], nk), "hr", new_sb[:, :]).then_inc(r_ready, 1)
                pe.wait_ge(hid_done, n + 1)
                project(at_step(ps_z[npar], nk), "hz", hid[:, par, k, :]).then_inc(z_ready, 1)
                t2 = k8 + 1 + LEAD
                if not last or k8 + 1 < 2 * STEPS - LEAD:
                    pe.wait_ge(h2_done, n)
                    project(at_step(ps_g, t2 % STEPS), "l2_h",
                            h2[:, (t2 - 1) // STEPS % 2, (t2 - 1) % STEPS, :]).then_inc(g_ready, 1)
                if k < STEPS - 1:
                    fill({0: 3, 1: 6, 2: 10}[k], pair, par, first, last_chunk, no_l2)
                else:
                    if not first:
                        pe.wait_ge(y_done, pair * 2 + par)
                    mm(ps_y, hid[:, par, :, :].rearrange("p s b -> p (s b)"), w("hq"), stop=False)

            pairs = CHUNKS // 2
            for k8 in range(2 * STEPS):
                step(0, k8, True, False)
            with pe.Fori(1, pairs - 1) as pair:
                for k8 in range(2 * STEPS):
                    step(pair, k8, False, False)
            for k8 in range(2 * STEPS):
                step(pairs - 1, k8, False, True)
            par = (CHUNKS - 1) % 2
            pe.wait_ge(hid_done, TIME + 1)
            pe.wait_ge(y_done, CHUNKS - 1)
            mm(ps_y, hid[:, par, :, :].rearrange("p s b -> p (s b)"), w("hq"), stop=False)
            mm(ps_y, x3[:, par, :], ident[:, :], start=False).then_inc(y_ready, 1)


def kernel(**inputs):
    import numpy as np
    import concourse.bacc as bacc
    from concourse.bass_utils import run_bass_kernel_spmd

    i = {k: np.asarray(v) for k, v in inputs.items()}
    n = N_STATE
    perm = np.array([g * BLOCK + (place - g * (BLOCK // GROUPS)) % BLOCK
                     for g in range(GROUPS) for place in range(BLOCK)])
    wp, l2w = i["L1_cond_Wp"], i["L2_cond_W"]
    twice = lambda a, axis: np.concatenate([a, a], axis=axis)
    squares = {
        "l0": i["L0_cond_weight"],
        "wp_b": twice(wp[:, :n], 1), "wp_c": twice(wp[:, n:], 1),
        "wpp_b": twice(wp[perm, :n], 1), "wpp_c": twice(wp[perm, n:], 1),
        "ws": twice(i["L1_cond_Ws"], 1), "wo": twice(i["L1_cond_Wo"], 0),
        "l2_h": l2w[:, :CH].T, "l2_z": l2w[:, CH:].T,
        "hr": i["L3_cond_Whr"].T, "hz": i["L3_cond_Whz"].T, "hh": i["L3_cond_Whh"].T,
        "xr": i["L3_cond_Wxr"].T, "xz": i["L3_cond_Wxz"].T, "xh": i["L3_cond_Wxh"].T,
        "hq": i["L3_cond_Whq"].T,
    }
    bp = i["L1_cond_bp"]
    columns = {
        "conv_b": i["L1_cond_conv_b"], "bp_b": twice(bp[:n], 0), "bp_c": twice(bp[n:], 0),
        "bs": twice(i["L1_cond_bs"], 0), "bo": i["L1_cond_bo"],
        "a_log": twice(i["L1_cond_A_log"], 0), "dt_log": twice(i["L1_cond_dt_log"], 0),
        "l2_b": i["L2_cond_b"], "alpha": i["L2_cond_alpha"],
        "bxr": i["L3_cond_bxr"], "bhr": i["L3_cond_bhr"], "bxz": i["L3_cond_bxz"],
        "bhz": i["L3_cond_bhz"], "bxh": i["L3_cond_bxh"], "bhh": i["L3_cond_bhh"],
    }
    arrays = {
        "x": np.ascontiguousarray(i["x"]),
        "cond": np.ascontiguousarray(i["cond_1024"]),
        "weights": np.ascontiguousarray(np.stack([squares[k] for k in WEIGHTS], axis=1)),
        "vectors": np.ascontiguousarray(np.stack([columns[k] for k in VECTORS], axis=1)),
        "bhq": np.ascontiguousarray(i["L3_cond_bhq"]),
    }
    nc = bacc.Bacc("TRN2", target_bir_lowering=False, num_devices=1)
    args = [nc.dram_tensor(k, a.shape, mybir.dt.from_np(a.dtype), kind="ExternalInput").ap()
            for k, a in arrays.items()]
    out = nc.dram_tensor("out", i["x"].shape, mybir.dt.float32, kind="ExternalOutput").ap()
    build(nc, *args, out)
    r = run_bass_kernel_spmd(nc, [arrays], core_ids=[0])
    return r.results[0]["out"]
```

```python
import concourse.bass as bass
from concourse import mybir
from contextlib import ExitStack

BATCH = 32
TIME = 128
CH = 128
N_STATE = 64
COLS = TIME * BATCH
STEPS = 4
CHUNK = STEPS * BATCH
CHUNKS = TIME // STEPS
BANK = 512
SLABS = COLS // BANK
BLOCK = 32
WINDOWS = TIME // BLOCK
WCOLS = BLOCK * BATCH
GROUPS = CH // BLOCK
ROWLEN = 2 * BLOCK
HALF_B = BATCH // 2
HALF_T = TIME // 2
FIRST_WEIGHTS = 4
LEAD = 6
EPS = 1e-8

WEIGHTS = ["l0", "ws", "wp_b", "wp_c", "wo", "l2_h", "l2_z",
           "hr", "hz", "hh", "xr", "xz", "xh", "hq"]
VECTORS = ["conv_b", "bp_b", "bp_c", "bs", "bo", "a_log", "dt_log", "l2_b", "alpha",
           "bxr", "bhr", "bxz", "bhz", "bxh", "bhh"]


def build(nc, x, cond, weights, vectors, bhq, out):
    f32 = mybir.dt.float32
    ACT = mybir.ActivationFunctionType
    ALU = mybir.AluOpType

    ctx = ExitStack()
    with ctx:
        def sb(name, shape):
            return ctx.enter_context(nc.sbuf_tensor(name, shape, f32))

        def sem(name):
            return ctx.enter_context(nc.semaphore(name))

        x_nat = sb("x_nat", [128, CHUNKS, CH])
        xT = sb("xT", [CH, COLS])
        xs = sb("xs", [CH, COLS])
        x1 = sb("x1", [CH, COLS])
        x1_win = sb("x1_win", [128, BLOCK, WINDOWS, BATCH])
        toep = sb("toep", [128, BLOCK, 2, 128])
        conv = sb("conv", [CH, COLS])
        soft = sb("soft", [128, TIME * HALF_B + 2])
        log_in = sb("log_in", [128, TIME * HALF_B + 2])
        u_sb = sb("u_sb", [128, TIME * HALF_B])
        gate_c = sb("gate_c", [128, TIME, HALF_B])
        decay_t = sb("decay_t", [128, HALF_B, HALF_T])
        room = toep[:, :, :, :].rearrange("p d v m -> p (d v m)")
        x2 = room[:, 0:COLS]
        third = TIME * HALF_B
        drive = room[:, COLS:COLS + third].rearrange("p (h b t) -> p h b t", h=2, b=HALF_B)
        state = room[:, COLS + third:COLS + 2 * third].rearrange("p (h b t) -> p h b t", h=2,
                                                                 b=HALF_B)
        gated = sb("gated", [128, TIME, HALF_B])
        w_sb = sb("w_sb", [128, len(WEIGHTS), 128])
        v_sb = sb("v_sb", [128, len(VECTORS)])
        bhq_rows = sb("bhq_rows", [128, CH])
        cond_nat = sb("cond_nat", [BATCH, CH])
        condT = sb("condT", [CH, BATCH])
        ysT = sb("ysT", [CH, BATCH])
        ys_sq = sb("ys_sq", [CH, BATCH])
        w0_sq = sb("w0_sq", [CH, CH])
        norm = sb("norm", [CH, 6, BATCH])
        dmod = sb("dmod", [CH, BATCH])
        filt = sb("filt", [CH, ROWLEN])
        filt_end = sb("filt_end", [1, ROWLEN])
        ident = sb("ident", [128, 128])
        flip = sb("flip", [BATCH, BATCH])
        ones = sb("ones", [128, BANK])
        proj_b = sb("proj_b", [128, 2])
        dt_a = sb("dt_a", [128, 2])
        leak = sb("leak", [CH, 1])
        gbias = sb("gbias", [CH, 3])
        dbias = sb("dbias", [CH, 4, CH])
        half = sb("half", [128, 1])
        warm = sb("warm", [128, 1])
        halved = sb("halved", [CH, 2, CH])
        r_sb = sb("r_sb", [CH, BATCH])
        z_sb = sb("z_sb", [CH, BATCH])
        q_sb = sb("q_sb", [CH, BATCH])
        zh_sb = sb("zh_sb", [CH, BATCH])
        omz_sb = sb("omz_sb", [CH, BATCH])
        cand_sb = sb("cand_sb", [CH, BATCH])
        new_sb = sb("new_sb", [CH, BATCH])
        hid = sb("hid", [CH, 2, STEPS, BATCH])
        g_sb = sb("g_sb", [CH, BATCH])
        gx_sb = sb("gx_sb", [CH, BATCH])
        s_sb = sb("s_sb", [CH, BATCH])
        h2 = sb("h2", [CH, 2, STEPS, BATCH])
        x3 = sb("x3", [CH, 2, CHUNK])
        y_sb = sb("y_sb", [128, 2, CH])

        filt_dram = nc.dram_tensor("filt_dram", [(CH + 1) * ROWLEN], f32, kind="Internal")

        ps = ctx.enter_context(nc.psum_tensor("ps", [128, 8, BANK], f32))
        ps_r = [ps[:, 0, 0:CHUNK], ps[:, 1, 0:CHUNK]]
        ps_z = [ps[:, 2, 0:CHUNK], ps[:, 3, 0:CHUNK]]
        ps_c = [ps[:, 4, 0:CHUNK], ps[:, 5, 0:CHUNK]]
        ps_g = ps[:, 6, 0:CHUNK]
        ps_y = ps[:, 7, 0:CHUNK]
        SMALL = 7
        PROJ_B = 2
        BANK_U = [4, 5, 6, 7]
        BANK_B = [4, 5, 0, 1]
        BANK_C = [6, 7, 2, 3]
        BANK_Y = [(4, 5), (6, 7), (0, 1), (2, 3)]

        def w(name):
            return w_sb[:, WEIGHTS.index(name), :]

        def vec(name):
            k = VECTORS.index(name)
            return v_sb[:, k:k + 1]

        dt = soft[:, TIME * HALF_B + 1:TIME * HALF_B + 2]
        SOFT_AD = slice(TIME * HALF_B, TIME * HALF_B + 2)

        ZERO_DVE = 12
        XS_DVE = 4

        def win(j):
            return slice(j * BANK, (j + 1) * BANK)

        def bcast(t, n):
            return t[:, :].rearrange("p (o b) -> p o b", o=1).to_broadcast([CH, n, BATCH])

        def tb(t, lo, n):
            return t[:, lo:lo + n].rearrange("p (t b) -> p t b", b=BATCH)

        ld_cond, ld_w0, ld_w, ld_w_rest, ld_v, ld_bhq = (
            sem(n) for n in ("ld_cond", "ld_w0", "ld_w", "ld_w_rest", "ld_v", "ld_bhq"))
        ld_x = [sem("ld_x_first_half"), sem("ld_x_second_half")]
        st_filt, ld_toep = sem("st_filt"), sem("ld_toep")
        toep_zero_dve, toep_zero_pool = sem("toep_zero_dve"), sem("toep_zero_pool")
        const_ready = sem("const_ready")
        cond_turned = sem("cond_turned")
        filt_done = sem("filt_done")
        ys_done, sq_done = sem("ys_done"), sem("sq_done")
        norm_mm, norm_in, norm_root, norm_step = (
            sem(n) for n in ("norm_mm", "norm_in", "norm_root", "norm_step"))
        x_turned, xT_done, xs_done, xs_pool_done, l0_mm, l0_scaled, x1_done = (
            sem(n) for n in ("x_turned", "xT_done", "xs_done", "xs_pool_done", "l0_mm", "l0_scaled", "x1_done"))
        win_done, conv_mm, conv_done = sem("win_done"), sem("conv_mm"), sem("conv_done")
        pb_mm, pb_done = sem("pb_mm"), sem("pb_done")
        relu_done, abs_done, tanh_done, log_done, soft_done = (
            sem(n) for n in ("relu_done", "abs_done", "tanh_done", "log_done", "soft_done"))
        decay_step, ad_relu, ad_abs, ad_tanh, ad_log = (
            sem(n) for n in ("decay_step", "ad_relu", "ad_abs", "ad_tanh", "ad_log"))
        u_mm, b_mm, c_mm, u_done = sem("u_mm"), sem("b_mm"), sem("c_mm"), sem("u_done")
        c_done = sem("c_done")
        carry_done = sem("carry_done")
        drive_done, scan_done, gated_done, y_mm, x2_done = (
            sem(n) for n in ("drive_done", "scan_done", "gated_done", "y_mm", "x2_done"))
        vec_done = sem("vec_done")
        pre_g, pre_sig, pre_gx, pre_s, pre_h = (
            sem(n) for n in ("pre_g", "pre_sig", "pre_gx", "pre_s", "pre_h"))
        r_ready, z_ready, c_ready, g_ready = (
            sem(n) for n in ("r_ready", "z_ready", "c_ready", "g_ready"))
        r_sig, z_sig, c_tanh, g_sig, h2_done = (
            sem(n) for n in ("r_sig", "z_sig", "c_tanh", "g_sig", "h2_done"))
        q_done, zh_done, omz_done, new_done, hid_done, gx_done, s_done = (
            sem(n) for n in ("q_done", "zh_done", "omz_done", "new_done", "hid_done", "gx_done",
                             "s_done"))
        x3_done, y_ready, y_done = sem("x3_done"), sem("y_ready"), sem("y_done")
        out_sent = [sem("out_sent_even"), sem("out_sent_odd")]

        out_v = out.rearrange("b (c s) d -> c s b d", s=STEPS)

        block = ctx.enter_context(nc.Block())

        @block.sync
        def _(sp_eng):
            sp_eng.dma_start(cond_nat[:, :], cond).then_inc(ld_cond, 16)
            x_v = x.rearrange("b (c s) d -> s b c d", s=STEPS)
            hc = CHUNKS // 2

            def load_x(half):
                for s in range(STEPS):
                    sp_eng.dma_start(x_nat[s * BATCH:(s + 1) * BATCH, half * hc:(half + 1) * hc, :],
                                     x_v[s, :, half * hc:(half + 1) * hc, :]).then_inc(ld_x[half], 16)

            load_x(0)
            sp_eng.wait_ge(filt_done, 2)
            sp_eng.dma_start(filt_dram[0:CH * ROWLEN].rearrange("(d m) -> d m", m=ROWLEN),
                             filt[:, :]).then_inc(st_filt, 16)
            sp_eng.dma_start(filt_dram[CH * ROWLEN:(CH + 1) * ROWLEN].rearrange("(o m) -> o m", o=1),
                             filt_end[:, :]).then_inc(st_filt, 16)
            load_x(1)
            sp_eng.dma_start(w_sb[:, 1:FIRST_WEIGHTS, :],
                             weights[:, 1:FIRST_WEIGHTS, :]).then_inc(ld_w, 16)
            sp_eng.wait_ge(st_filt, 32)
            sp_eng.wait_ge(toep_zero_dve, 1)
            sp_eng.wait_ge(toep_zero_pool, 1)
            for g in range(GROUPS):
                src = bass.AP(filt_dram, g * BLOCK * ROWLEN,
                              [[1, BLOCK], [ROWLEN, BLOCK], [BLOCK, 2], [1, BLOCK]])
                rows = slice(g * BLOCK, (g + 1) * BLOCK)
                sp_eng.dma_start(toep[rows, :, :, rows], src).then_inc(ld_toep, 16)
            sp_eng.dma_start(w_sb[:, FIRST_WEIGHTS:, :],
                             weights[:, FIRST_WEIGHTS:, :]).then_inc(ld_w_rest, 16)
            sp_eng.dma_start(bhq_rows[:, :], bhq.rearrange("(o n) -> o n", o=1)
                             .to_broadcast([128, CH])).then_inc(ld_bhq, 16)

            def send(pair, par, c):
                sp_eng.wait_ge(y_done, c + 1)
                sp_eng.dma_start(out_v[bass.ds(c, 1), :, :, :].rearrange("o s b d -> (o s) b d"),
                                 y_sb[:, par, :]).then_inc(out_sent[par], 16)

            with sp_eng.Fori(0, CHUNKS // 2) as pair:
                send(pair, 0, pair * 2)
                send(pair, 1, pair * 2 + 1)
            for par in range(2):
                sp_eng.wait_ge(out_sent[par], 16 * (CHUNKS // 2 + par))

        @block.gpsimd
        def _(pool):
            nc.gpsimd.memset(ident[:, :], 0.0).then_inc(const_ready, 1)
            nc.gpsimd.memset(flip[:, :], 0.0).then_inc(const_ready, 1)
            pool.wait_ge(const_ready, 2)
            nc.gpsimd.affine_select(out=ident[:, :], in_=ident[:, :], compare_op=ALU.not_equal,
                                    fill=1.0, base=0, pattern=[[-1, 128]],
                                    channel_multiplier=1).then_inc(const_ready, 1)
            nc.gpsimd.affine_select(out=flip[:, :], in_=flip[:, :], compare_op=ALU.not_equal,
                                    fill=1.0, base=1 - BATCH, pattern=[[1, BATCH]],
                                    channel_multiplier=1).then_inc(const_ready, 1)
            nc.gpsimd.memset(ones[:, :], 1.0).then_inc(const_ready, 1)
            nc.gpsimd.memset(filt[:, :], 0.0).then_inc(const_ready, 1)
            nc.gpsimd.memset(filt_end[:, :], 0.0).then_inc(const_ready, 1)
            nc.gpsimd.memset(half[:, :], 0.5).then_inc(const_ready, 1)
            nc.gpsimd.memset(decay_t[:, :, :], 1.0).then_inc(const_ready, 1)
            pool.wait_ge(const_ready, 9)
            nc.gpsimd.memset(decay_t[:, :, 0:1], 0.0).then_inc(const_ready, 1)
            nc.gpsimd.memset(toep[:, ZERO_DVE:, :, :], 0.0).then_inc(toep_zero_pool, 1)
            pool.wait_ge(ys_done, 2)
            for q in range(XS_DVE, SLABS):
                pool.wait_ge(xT_done, q + 1)
                nc.gpsimd.tensor_tensor(tb(xs, q * BANK, BANK), tb(xT, q * BANK, BANK),
                                        bcast(ysT, BANK // BATCH), ALU.mult).then_inc(xs_pool_done, 1)

        @block.scalar
        def _(act):
            act.dma_start(w_sb[:, 0, :], weights[:, 0, :]).then_inc(ld_w0, 16)
            act.dma_start(v_sb[:, :], vectors).then_inc(ld_v, 16)
            act.wait_ge(norm_in, 1)
            nc.scalar.activation(norm[:, 1, :], norm[:, 0, :], ACT.Sqrt).then_inc(norm_root, 1)
            k_log = VECTORS.index("a_log")
            log_pair = v_sb[:, k_log:k_log + 2]

            def decay_parts():
                act.wait_ge(ld_v, 16)
                nc.scalar.activation(soft[:, SOFT_AD], log_pair, ACT.Relu).then_inc(ad_relu, 1)
                nc.scalar.activation(log_in[:, SOFT_AD], log_pair, ACT.Abs).then_inc(ad_abs, 1)
                act.wait_ge(ad_abs, 1)
                nc.scalar.activation(log_in[:, SOFT_AD], log_in[:, SOFT_AD], ACT.Tanh,
                                     scale=0.5).then_inc(ad_tanh, 1)
                act.wait_ge(ad_tanh, 1)
                nc.scalar.activation(log_in[:, SOFT_AD], log_in[:, SOFT_AD], ACT.Ln,
                                     scale=0.5, bias=half[:, 0:1]).then_inc(ad_log, 1)
                nc.scalar.activation(warm[:, :], half[:, :], ACT.Tanh)

            def copy_u(j):
                act.wait_ge(u_mm, j + 1)
                nc.scalar.activation(u_sb[:, win(j)], ps[:, BANK_U[j], :], ACT.Identity,
                                     bias=vec("bs")).then_inc(u_done, 1)

            act.wait_ge(const_ready, 8)
            for q in range(SLABS):
                act.wait_ge(x_turned, q + 1)
                nc.scalar.activation(xT[:, q * BANK:(q + 1) * BANK], ps[:, q % 2, :],
                                     ACT.Copy).then_inc(xT_done, 1)
                if q == SLABS // 2:
                    decay_parts()
                if q == SLABS // 2 + 2:
                    copy_u(0)
            for j in range(1, WINDOWS):
                copy_u(j)

            def absolute(j):
                act.wait_ge(b_mm, j + 1)
                nc.scalar.activation(log_in[:, win(j)], ps[:, BANK_B[j], :], ACT.Abs,
                                     bias=proj_b[:, 0:1]).then_inc(abs_done, 1)

            def tanh_b(j):
                act.wait_ge(abs_done, j + 1)
                nc.scalar.activation(log_in[:, win(j)], log_in[:, win(j)], ACT.Tanh,
                                     scale=0.5).then_inc(tanh_done, 1)

            def log_b(j):
                act.wait_ge(tanh_done, j + 1)
                nc.scalar.activation(log_in[:, win(j)], log_in[:, win(j)], ACT.Ln,
                                     scale=0.5, bias=half[:, 0:1]).then_inc(log_done, 1)

            def tanh_c(j):
                act.wait_ge(c_mm, j + 1)
                nc.scalar.activation(gate_c[:, j * BLOCK:(j + 1) * BLOCK, :], ps[:, BANK_C[j], :]
                                     .rearrange("p (t b) -> p t b", b=HALF_B), ACT.Tanh,
                                     bias=proj_b[:, 1:2]).then_inc(c_done, 1)

            def lead_step(t):
                act.wait_ge(pre_g, t + 1)
                nc.scalar.activation(g_sb[:, :], ps_g[:, (t % STEPS) * BATCH:(t % STEPS + 1) * BATCH],
                                     ACT.Tanh, scale=0.5).then_inc(pre_sig, 1)
                act.wait_ge(pre_s, t + 1)
                nc.scalar.activation(h2[:, t // STEPS % 2, t % STEPS, :], s_sb[:, :],
                                     ACT.Tanh, scale=0.5).then_inc(pre_h, 1)

            act.wait_ge(pb_done, 2)
            for j in range(WINDOWS):
                absolute(j)
                tanh_b(j)
            for j in range(WINDOWS):
                log_b(j)
            for j in range(WINDOWS):
                tanh_c(j)
            for t in range(LEAD):
                lead_step(t)

            def step(n, k8, l2):
                par, k = k8 // STEPS, k8 % STEPS
                here = slice(k * BATCH, (k + 1) * BATCH)
                par2, k2 = (k8 + LEAD) // STEPS % 2, (k8 + LEAD) % STEPS
                act.wait_ge(r_ready, n)
                nc.scalar.activation(r_sb[:, :], ps_r[par][:, here], ACT.Tanh,
                                     scale=0.5).then_inc(r_sig, 1)
                act.wait_ge(z_ready, n)
                nc.scalar.activation(z_sb[:, :], ps_z[par][:, here], ACT.Tanh,
                                     scale=0.5).then_inc(z_sig, 1)
                if l2:
                    act.wait_ge(g_ready, n)
                    nc.scalar.activation(g_sb[:, :], ps_g[:, k2 * BATCH:(k2 + 1) * BATCH],
                                         ACT.Tanh, scale=0.5).then_inc(g_sig, 1)
                act.wait_ge(c_ready, n)
                nc.scalar.activation(cand_sb[:, :], ps_c[par][:, here], ACT.Tanh).then_inc(c_tanh, 1)
                if l2:
                    act.wait_ge(s_done, n)
                    nc.scalar.activation(h2[:, par2, k2, :], s_sb[:, :], ACT.Tanh,
                                         scale=0.5).then_inc(h2_done, 1)

            pairs = CHUNKS // 2
            with act.Fori(0, pairs - 1) as pair:
                for k8 in range(2 * STEPS):
                    step(pair * (2 * STEPS) + (k8 + 1), k8, True)
            for k8 in range(2 * STEPS):
                step((pairs - 1) * 2 * STEPS + k8 + 1, k8, k8 < 2 * STEPS - LEAD)

        @block.vector
        def _(dve):
            nc.vector.memset(toep[:, 0:ZERO_DVE, :, :], 0.0).then_inc(toep_zero_dve, 1)
            dve.wait_ge(cond_turned, 2)
            dve.wait_ge(const_ready, 7)
            nc.vector.tensor_copy(filt[:, BLOCK - 1:2 * BLOCK - 1],
                                  ps[:, SMALL, BATCH:2 * BATCH]).then_inc(filt_done, 2)
            nc.vector.tensor_copy(condT[:, :], ps[:, SMALL, 0:BATCH]).then_inc(ys_done, 1)
            nc.vector.tensor_scalar(ysT[:, :], ps[:, SMALL, 0:BATCH], float(CH) ** -0.5, None,
                                    ALU.mult).then_inc(ys_done, 1)
            dve.wait_ge(ys_done, 2)
            nc.vector.tensor_tensor(ys_sq[:, :], ysT[:, :], ysT[:, :], ALU.mult).then_inc(sq_done, 1)
            dve.wait_ge(ld_w0, 16)
            nc.vector.tensor_tensor(w0_sq[:, :], w("l0"), w("l0"), ALU.mult).then_inc(sq_done, 1)
            dve.wait_ge(norm_mm, 1)
            nc.vector.tensor_scalar(norm[:, 0, :], ps[:, SMALL, 2 * BATCH:3 * BATCH], EPS, None,
                                    ALU.add).then_inc(norm_in, 1)
            dve.wait_ge(norm_root, 1)
            nc.vector.reciprocal(norm[:, 2, :], norm[:, 1, :]).then_inc(norm_step, 1)
            dve.wait_ge(norm_step, 1)
            nc.vector.tensor_tensor(norm[:, 3, :], norm[:, 2, :], norm[:, 2, :],
                                    ALU.mult).then_inc(norm_step, 1)
            dve.wait_ge(norm_step, 2)
            nc.vector.tensor_tensor(norm[:, 4, :], norm[:, 3, :], norm[:, 0, :],
                                    ALU.mult).then_inc(norm_step, 1)
            dve.wait_ge(norm_step, 3)
            nc.vector.tensor_scalar(norm[:, 5, :], norm[:, 4, :], -0.5, 1.5, ALU.mult,
                                    ALU.add).then_inc(norm_step, 1)
            dve.wait_ge(norm_step, 4)
            nc.vector.tensor_tensor(dmod[:, :], norm[:, 2, :], norm[:, 5, :],
                                    ALU.mult).then_inc(norm_step, 1)
            dve.wait_ge(norm_step, 5)

            slab_t = BANK // BATCH

            def finish_x1(q):
                lo = q * BANK
                dve.wait_ge(l0_mm, q + 1)
                nc.vector.tensor_tensor(tb(x1, lo, BANK), ps[:, 2 + q % 2, :]
                                        .rearrange("p (t b) -> p t b", b=BATCH),
                                        bcast(dmod, slab_t), ALU.mult).then_inc(l0_scaled, 1)
                dve.wait_ge(l0_scaled, q + 1)
                nc.vector.tensor_tensor(x1[:, lo:lo + BANK], x1[:, lo:lo + BANK],
                                        xT[:, lo:lo + BANK], ALU.add).then_inc(x1_done, 1)

            def window(j):
                dve.wait_ge(x1_done, (j + 1) * SLABS // WINDOWS)
                nc.vector.transpose(
                    x1_win[:, :, j, :].rearrange("p d b -> p b d"),
                    tb(x1, j * WCOLS, WCOLS)[:, ::-1, :].rearrange("p t b -> p b t")
                ).then_inc(win_done, 1)

            def scale_x(q):
                dve.wait_ge(xT_done, q + 1)
                nc.vector.tensor_tensor(tb(xs, q * BANK, BANK), tb(xT, q * BANK, BANK),
                                        bcast(ysT, slab_t), ALU.mult).then_inc(xs_done, 1)

            scale_x(0)
            for q in range(SLABS):
                if q + 1 < XS_DVE:
                    scale_x(q + 1)
                finish_x1(q)
                if q == 4:
                    window(0)
                if q == 6:
                    window(1)
            window(2)
            window(3)
            dve.wait_ge(ld_v, 16)
            dve.wait_ge(pb_mm, 2)
            nc.vector.tensor_tensor(proj_b[:, 0:1], ps[:, PROJ_B, 0:1], vec("bp_b"),
                                    ALU.add).then_inc(pb_done, 1)
            nc.vector.tensor_tensor(proj_b[:, 1:2], ps[:, PROJ_B, 1:2], vec("bp_c"),
                                    ALU.add).then_inc(pb_done, 1)
            dve.wait_ge(const_ready, 10)
            nc.vector.tensor_scalar(leak[:, :], vec("alpha"), -2.0, 2.0, ALU.mult,
                                    ALU.add).then_inc(vec_done, 1)
            for k, gate in enumerate(("r", "z", "h")):
                nc.vector.tensor_tensor(gbias[:, k:k + 1], vec("bx" + gate), vec("bh" + gate),
                                        ALU.add).then_inc(vec_done, 1)
            dve.wait_ge(vec_done, 4)
            for k in range(3):
                nc.vector.tensor_scalar(dbias[:, k, :], ident[:, :], gbias[:, k:k + 1], None,
                                        ALU.mult).then_inc(vec_done, 1)
            nc.vector.tensor_scalar(dbias[:, 3, :], ident[:, :], vec("l2_b"), None,
                                    ALU.mult).then_inc(vec_done, 1)
            def turn_back(j):
                dve.wait_ge(conv_mm, 1)
                src = ps[:, :, :].rearrange("p a (m j b) -> p j b (a m)", j=WINDOWS, b=BATCH)
                nc.vector.transpose(tb(conv, j * WCOLS, WCOLS).rearrange("p t b -> p b t"),
                                    src[:, j, :, :]).then_inc(conv_done, 1)

            def relu_b(j):
                dve.wait_ge(abs_done, j + 1)
                nc.vector.tensor_scalar(soft[:, win(j)], ps[:, BANK_B[j], :], proj_b[:, 0:1], 0.0,
                                        ALU.add, ALU.max).then_inc(relu_done, 1)

            def half_cols(j):
                return slice(j % 2 * BLOCK, (j % 2 + 1) * BLOCK)

            def drive_window(j):
                dve.wait_ge(log_done, j + 1)
                dve.wait_ge(relu_done, j + 1)
                nc.vector.tensor_tensor(soft[:, win(j)], soft[:, win(j)], log_in[:, win(j)],
                                        ALU.subtract).then_inc(soft_done, 1)
                dve.wait_ge(soft_done, j + 2)
                dve.wait_ge(u_done, j + 1)
                nc.vector.tensor_tensor(
                    drive[:, j // 2, :, half_cols(j)].rearrange("p b t -> p t b"),
                    u_sb[:, win(j)].rearrange("p (t b) -> p t b", b=HALF_B),
                    soft[:, win(j)].rearrange("p (t b) -> p t b", b=HALF_B),
                    ALU.mult).then_inc(drive_done, 1)

            def scan(h):
                dve.wait_ge(drive_done, 2 * (h + 1))
                if h == 1:
                    nc.vector.scalar_tensor_tensor(
                        out=drive[:, 1, :, 0:1], in0=state[:, 0, :, HALF_T - 1:HALF_T],
                        scalar=dt_a[:, 1:2], in1=drive[:, 1, :, 0:1],
                        op0=ALU.mult, op1=ALU.add).then_inc(carry_done, 1)
                    dve.wait_ge(carry_done, 1)
                nc.vector.tensor_tensor_scan(state[:, h, :, :].rearrange("p b t -> p (b t)"),
                                             decay_t[:, :, :].rearrange("p b t -> p (b t)"),
                                             drive[:, h, :, :].rearrange("p b t -> p (b t)"),
                                             0.0, ALU.mult, ALU.add).then_inc(scan_done, 1)

            def gate_window(j):
                dve.wait_ge(c_done, j + 1)
                dve.wait_ge(scan_done, j // 2 + 1)
                nc.vector.scalar_tensor_tensor(
                    out=gated[:, j * BLOCK:(j + 1) * BLOCK, :],
                    in0=state[:, j // 2, :, half_cols(j)].rearrange("p b t -> p t b"),
                    scalar=dt, in1=gate_c[:, j * BLOCK:(j + 1) * BLOCK, :],
                    op0=ALU.mult, op1=ALU.mult).then_inc(gated_done, 1)

            def x2_window(j):
                dve.wait_ge(y_mm, j + 1)
                for hb in range(2):
                    cols = slice(hb * HALF_B, (hb + 1) * HALF_B)
                    nc.vector.scalar_tensor_tensor(
                        out=tb(x2, j * WCOLS, WCOLS)[:, :, cols],
                        in0=ps[:, BANK_Y[j][hb], :].rearrange("p (t b) -> p t b", b=HALF_B),
                        scalar=vec("bo"), in1=tb(x1, j * WCOLS, WCOLS)[:, :, cols],
                        op0=ALU.add, op1=ALU.add).then_inc(x2_done, 1)

            def lead_step(t):
                dve.wait_ge(pre_sig, t + 1)
                nc.vector.scalar_tensor_tensor(
                    out=gx_sb[:, :], in0=g_sb[:, :], scalar=1.0, in1=x2[:, t * BATCH:(t + 1) * BATCH],
                    op0=ALU.add, op1=ALU.mult).then_inc(pre_gx, 1)
                dve.wait_ge(pre_gx, t + 1)
                nc.vector.scalar_tensor_tensor(
                    out=s_sb[:, :], in0=h2[:, (t - 1) // STEPS % 2, (t - 1) % STEPS, :],
                    scalar=leak[:, :], in1=gx_sb[:, :], op0=ALU.mult, op1=ALU.add
                ).then_inc(pre_s, 1)
                if t % STEPS == STEPS - 1:
                    c = t // STEPS
                    dve.wait_ge(pre_h, t + 2)
                    nc.vector.tensor_tensor(x3[:, c % 2, :], x2[:, c * CHUNK:(c + 1) * CHUNK],
                                            h2[:, c % 2, :, :].rearrange("p s b -> p (s b)"),
                                            ALU.add).then_inc(x3_done, 1)

            dve.wait_ge(ld_w_rest, 16)
            for k, name in enumerate(("hr", "hh")):
                nc.vector.tensor_scalar(halved[:, k, :], w(name), 0.5, None,
                                        ALU.mult).then_inc(vec_done, 1)
            dve.wait_ge(ad_log, 1)
            nc.vector.tensor_tensor(soft[:, SOFT_AD], soft[:, SOFT_AD], log_in[:, SOFT_AD],
                                    ALU.subtract).then_inc(soft_done, 1)
            dve.wait_ge(soft_done, 1)
            nc.vector.tensor_tensor(dt_a[:, 0:1], soft[:, SOFT_AD.start:SOFT_AD.start + 1], dt,
                                    ALU.mult).then_inc(decay_step, 1)
            dve.wait_ge(decay_step, 1)
            nc.vector.tensor_scalar(dt_a[:, 1:2], dt_a[:, 0:1], -1.0, 1.0, ALU.mult,
                                    ALU.add).then_inc(decay_step, 1)
            dve.wait_ge(decay_step, 2)
            nc.vector.tensor_scalar(decay_t[:, :, :], decay_t[:, :, :], dt_a[:, 1:2], None,
                                    ALU.mult).then_inc(decay_step, 1)
            dve.wait_ge(pb_done, 2)
            dve.wait_ge(decay_step, 3)
            for j in range(WINDOWS):
                turn_back(j)
            for j in range(WINDOWS):
                relu_b(j)
            drive_window(0)
            drive_window(1)
            scan(0)
            gate_window(0)
            gate_window(1)
            dve.wait_ge(ys_done, 2)
            nc.vector.tensor_copy(h2[:, 1, STEPS - 1, :], condT[:, :]).then_inc(pre_h, 1)
            nc.vector.tensor_copy(hid[:, 1, STEPS - 1, :], condT[:, :]).then_inc(hid_done, 1)
            drive_window(2)
            x2_window(0)
            x2_window(1)
            dve.wait_ge(pre_h, 1)
            dve.wait_ge(x2_done, 2)
            drive_window(3)
            scan(1)
            lead_step(0)
            gate_window(2)
            gate_window(3)
            lead_step(1)
            lead_step(2)
            x2_window(2)
            lead_step(3)
            x2_window(3)
            lead_step(4)
            lead_step(5)
            dve.wait_ge(x2_done, 2 * WINDOWS)
            dve.wait_ge(ld_bhq, 16)
            nc.vector.memset(y_sb[:, 1, :], 0.0).then_inc(out_sent[1], 16)

            def send_y(c, par, sent):
                if not isinstance(sent, int) or sent > 0:
                    dve.wait_ge(out_sent[par], sent)
                dve.wait_ge(y_ready, c + 1)
                nc.vector.tensor_tensor(y_sb[:, par, :], ps_y, bhq_rows[:, :],
                                        ALU.add).then_inc(y_done, 1)

            def step(n, t_off, k8, l2, out_chunk, out_count):
                par, k = k8 // STEPS, k8 % STEPS
                prev = hid[:, (k8 - 1) // STEPS % 2, (k8 - 1) % STEPS, :]
                t2 = k8 + LEAD
                par2, k2 = t2 // STEPS % 2, t2 % STEPS
                prev2 = h2[:, (t2 - 1) // STEPS % 2, (t2 - 1) % STEPS, :]
                dve.wait_ge(r_sig, n)
                dve.wait_ge(hid_done, n)
                nc.vector.scalar_tensor_tensor(out=q_sb[:, :], in0=r_sb[:, :], scalar=1.0, in1=prev,
                                               op0=ALU.add, op1=ALU.mult).then_inc(q_done, 1)
                dve.wait_ge(z_sig, n)
                nc.vector.scalar_tensor_tensor(out=zh_sb[:, :], in0=z_sb[:, :], scalar=1.0, in1=prev,
                                               op0=ALU.add, op1=ALU.mult).then_inc(zh_done, 1)
                nc.vector.tensor_scalar(omz_sb[:, :], z_sb[:, :], -0.5, 0.5, ALU.mult,
                                        ALU.add).then_inc(omz_done, 1)
                if l2:
                    dve.wait_ge(g_sig, n)
                    col = t_off + (k8 + LEAD) * BATCH
                    nc.vector.scalar_tensor_tensor(
                        out=gx_sb[:, :], in0=g_sb[:, :], scalar=1.0, in1=x2[:, bass.ds(col, BATCH)],
                        op0=ALU.add, op1=ALU.mult).then_inc(gx_done, 1)
                    dve.wait_ge(gx_done, n)
                    nc.vector.scalar_tensor_tensor(out=s_sb[:, :], in0=prev2, scalar=leak[:, :],
                                                   in1=gx_sb[:, :], op0=ALU.mult,
                                                   op1=ALU.add).then_inc(s_done, 1)
                dve.wait_ge(c_tanh, n)
                dve.wait_ge(omz_done, n)
                nc.vector.tensor_tensor(new_sb[:, :], omz_sb[:, :], cand_sb[:, :],
                                        ALU.mult).then_inc(new_done, 1)
                dve.wait_ge(new_done, n)
                nc.vector.scalar_tensor_tensor(out=hid[:, par, k, :], in0=zh_sb[:, :], scalar=0.5,
                                               in1=new_sb[:, :], op0=ALU.mult,
                                               op1=ALU.add).then_inc(hid_done, 1)
                if k == 1 and out_count is not None:
                    send_y(out_chunk, 1 - par, out_count)
                if l2 and k2 == STEPS - 1:
                    dve.wait_ge(h2_done, n)
                    lo = t_off + (k8 + LEAD - (STEPS - 1)) * BATCH
                    nc.vector.tensor_tensor(x3[:, par2, :], x2[:, bass.ds(lo, CHUNK)],
                                            h2[:, par2, :, :].rearrange("p s b -> p (s b)"),
                                            ALU.add).then_inc(x3_done, 1)

            pairs = CHUNKS // 2

            def chunk_pair(pair, peeled, last):
                for k8 in range(2 * STEPS):
                    par = k8 // STEPS
                    out_chunk = pair * 2 + (par - 1)
                    out_count = None if peeled and par == 0 else pair * 16
                    step(pair * (2 * STEPS) + (k8 + 1), pair * (2 * CHUNK), k8,
                         not last or k8 < 2 * STEPS - LEAD, out_chunk, out_count)

            chunk_pair(0, True, False)
            with dve.Fori(1, pairs - 1) as pair:
                chunk_pair(pair, False, False)
            chunk_pair(pairs - 1, False, True)
            send_y(CHUNKS - 1, 1, 16 * pairs)

        @block.tensor
        def _(pe):
            def mm(o, lhsT, rhs, start=True, stop=True):
                return nc.tensor.matmul(o, lhsT, rhs, start=start, stop=stop, skip_group_check=True)

            def keep_streaming(o, times=1):
                for _ in range(times):
                    mm(o, ident[:, :], ones[:, 0:o.shape[-1]])

            FREE = 4
            pe.wait_ge(const_ready, 5)
            keep_streaming(ps[:, FREE, 0:CHUNK], 3)
            pe.wait_ge(ld_cond, 16)
            nc.tensor.transpose(ps[:, SMALL, 0:BATCH], cond_nat[:, :],
                                ident[0:BATCH, 0:BATCH]).then_inc(cond_turned, 1)
            nc.tensor.transpose(ps[:, SMALL, BATCH:2 * BATCH], cond_nat[:, :],
                                flip[:, :]).then_inc(cond_turned, 1)
            keep_streaming(ps[:, FREE, 0:CHUNK], 3)
            pe.wait_ge(ys_done, 2)
            pe.wait_ge(sq_done, 2)
            mm(ps[:, SMALL, 2 * BATCH:3 * BATCH], w0_sq[:, :], ys_sq[:, :]).then_inc(norm_mm, 1)

            keep_streaming(ps[:, FREE, 0:CHUNK], 5)
            per = BANK // CHUNK

            def turn_x(q):
                if q == 0:
                    pe.wait_ge(ld_x[0], 16 * STEPS)
                if q == SLABS // 2:
                    pe.wait_ge(ld_x[1], 16 * STEPS)
                if q >= 2:
                    pe.wait_ge(xT_done, q - 1)
                for i in range(per):
                    last = nc.tensor.transpose(ps[:, q % 2, i * CHUNK:(i + 1) * CHUNK],
                                               x_nat[:, q * per + i, :], ident[:, :])
                last.then_inc(x_turned, 1)

            def l0(q):
                if q < XS_DVE:
                    pe.wait_ge(xs_done, q + 1)
                else:
                    pe.wait_ge(xs_pool_done, q + 1 - XS_DVE)
                if q >= 2:
                    pe.wait_ge(l0_scaled, q - 1)
                mm(ps[:, 2 + q % 2, :], w("l0"), xs[:, q * BANK:(q + 1) * BANK]).then_inc(l0_mm, 1)

            def conv_channel(i):
                bank, at = i // per, i % per * CHUNK
                rhs = x1_win[:, i, :, :].rearrange("p j b -> p (j b)")
                mm(ps[:, bank, at:at + CHUNK], toep[:, i, 0, :], rhs, stop=False)
                return mm(ps[:, bank, at + BATCH:at + CHUNK], toep[:, i, 1, :],
                          rhs[:, 0:(WINDOWS - 1) * BATCH], start=False)

            def batch_halves(name, src, j, bank, done):
                for hb in range(2):
                    rhs = tb(src, j * WCOLS, WCOLS)[:, :, hb * HALF_B:(hb + 1) * HALF_B]
                    last = mm(ps[hb * N_STATE:(hb + 1) * N_STATE, bank, :],
                              w(name)[:, 0:N_STATE], rhs)
                last.then_inc(done, 1)

            def project_b(j):
                if j == 0:
                    pe.wait_ge(conv_done, WINDOWS)
                batch_halves("wp_b", conv, j, BANK_B[j], b_mm)

            def project_c(j):
                batch_halves("wp_c", conv, j, BANK_C[j], c_mm)

            def project_y(j):
                pe.wait_ge(gated_done, j + 1)
                if j % 2 == 0:
                    pe.wait_ge(relu_done, j + 2)
                else:
                    pe.wait_ge(c_done, j + 1)
                for swap in range(2):
                    for hb in range(2):
                        rows = slice(hb * N_STATE, (hb + 1) * N_STATE)
                        outs = slice((hb ^ swap) * N_STATE, ((hb ^ swap) + 1) * N_STATE)
                        last = mm(ps[outs, BANK_Y[j][hb], :], w("wo")[rows, outs],
                                  gated[rows, j * BLOCK:(j + 1) * BLOCK, :]
                                  .rearrange("p t b -> p (t b)"))
                last.then_inc(y_mm, 1)

            turn_x(0)
            for q in range(SLABS):
                if q + 1 < SLABS:
                    turn_x(q + 1)
                if q % 2 == 0 and q >= 4:
                    j = q // 2 - 2
                    if j == 0:
                        pe.wait_ge(ld_w, 16)
                    pe.wait_ge(x1_done, 2 * (j + 1))
                    batch_halves("ws", x1, j, BANK_U[j], u_mm)
                l0(q)
                if q < 4:
                    keep_streaming(ps[:, FREE, 0:CHUNK], 1)
            for j in (2, 3):
                pe.wait_ge(x1_done, 2 * (j + 1))
                batch_halves("ws", x1, j, BANK_U[j], u_mm)
            pe.wait_ge(ld_v, 16)
            pe.wait_ge(l0_scaled, SLABS)
            for k, name in enumerate(("wp_b", "wp_c")):
                mm(ps[:, PROJ_B, k:k + 1], w(name), vec("conv_b")).then_inc(pb_mm, 1)
            keep_streaming(ps[:, 0, :], 2)

            pe.wait_ge(win_done, WINDOWS)
            pe.wait_ge(ld_toep, 16 * GROUPS)
            pe.wait_ge(u_done, WINDOWS)
            pe.wait_ge(pb_done, 2)
            for i in range(BLOCK):
                last = conv_channel(i)
            last.then_inc(conv_mm, 1)
            for j in range(WINDOWS):
                project_b(j)
            for j in range(WINDOWS):
                project_c(j)
            pe.wait_ge(ld_w_rest, 16)
            project_y(0)
            project_y(1)

            DIAG = {"r": 0, "z": 1, "h": 2, "g": 3}

            def bias(o, gate):
                return mm(o, dbias[:, DIAG[gate], :], ones[:, 0:CHUNK], stop=False)

            def project(o, name, rhs):
                return mm(o, w(name), rhs, start=False)

            def project_twice(o, name, rhs):
                return mm(o, halved[:, ("hr", "hh").index(name), :], rhs, start=False)

            def at_step(o, k):
                return o[:, k * BATCH:(k + 1) * BATCH]

            pe.wait_ge(vec_done, 10)
            pe.wait_ge(x2_done, 4)
            def lead_step(t):
                if t % STEPS == 0:
                    if t:
                        pe.wait_ge(pre_sig, t)
                    bias(ps_g, "g")
                    project(ps_g, "l2_z", x2[:, t * BATCH:t * BATCH + CHUNK])
                pe.wait_ge(pre_h, t + 1)
                project(at_step(ps_g, t % STEPS), "l2_h",
                        h2[:, (t - 1) // STEPS % 2, (t - 1) % STEPS, :]).then_inc(pre_g, 1)

            spare = ps[:, 7, :]
            lead_step(0)
            keep_streaming(spare, 2)
            lead_step(1)
            keep_streaming(spare, 2)
            project_y(2)
            lead_step(2)
            project_y(3)
            lead_step(3)
            keep_streaming(spare, 2)
            lead_step(4)
            keep_streaming(spare, 1)
            pe.wait_ge(x3_done, 1)
            pe.wait_ge(x2_done, 2 * WINDOWS)
            for gate, o in (("r", ps_r), ("z", ps_z), ("h", ps_c)):
                bias(o[0], gate)
                project(o[0], "x" + gate, x3[:, 0, :])
            lead_step(5)

            pe.wait_ge(hid_done, 1)
            h_init = hid[:, 1, STEPS - 1, :]
            project(at_step(ps_r[0], 0), "hr", h_init).then_inc(r_ready, 1)
            project(at_step(ps_z[0], 0), "hz", h_init).then_inc(z_ready, 1)
            pe.wait_ge(pre_h, LEAD + 1)
            project(at_step(ps_g, LEAD % STEPS), "l2_h",
                    h2[:, (LEAD - 1) // STEPS % 2, (LEAD - 1) % STEPS, :]).then_inc(g_ready, 1)

            def fill(slot, pair, par, first, last_chunk, no_l2):
                nxt = 1 - par
                if slot == 1 and not first:
                    mm(ps_y, x3[:, nxt, :], ident[:, :], start=False).then_inc(y_ready, 1)
                elif slot > 9 or last_chunk or slot == 1 or (slot in (4, 5) and no_l2):
                    if slot > 9 and not last_chunk:
                        if not first:
                            pe.wait_ge(y_done, pair * 2 + par)
                        keep_streaming(ps_y)
                    else:
                        keep_streaming(ps_c[nxt])
                if last_chunk:
                    return
                if slot == 2:
                    bias(ps_r[nxt], "r")
                if slot == 3:
                    bias(ps_z[nxt], "z")
                if slot == 4 and not no_l2:
                    pe.wait_ge(g_sig, pair * (2 * STEPS) + (par * STEPS + 2))
                    bias(ps_g, "g")
                if slot == 5 and not no_l2:
                    lo = pair * (2 * CHUNK) + (par + 2) * CHUNK
                    project(ps_g, "l2_z", x2[:, bass.ds(lo, CHUNK)])
                if slot == 6:
                    bias(ps_c[nxt], "h")
                if slot == 7:
                    pe.wait_ge(x3_done, pair * 2 + (par + 2))
                    project(ps_r[nxt], "xr", x3[:, nxt, :])
                if slot == 8:
                    project(ps_z[nxt], "xz", x3[:, nxt, :])
                if slot == 9:
                    project(ps_c[nxt], "xh", x3[:, nxt, :])

            def step(pair, k8, peeled, last):
                par, k = k8 // STEPS, k8 % STEPS
                n = pair * (2 * STEPS) + (k8 + 1)
                first = peeled and par == 0
                last_chunk = last and par == 1
                no_l2 = last
                nxt8 = (k8 + 1) % (2 * STEPS)
                npar, nk = nxt8 // STEPS, nxt8 % STEPS
                if last and k8 == 2 * STEPS - 1:
                    pe.wait_ge(q_done, n)
                    project_twice(at_step(ps_c[par], k), "hh", q_sb[:, :]).then_inc(c_ready, 1)
                    return
                pe.wait_ge(q_done, n)
                project_twice(at_step(ps_c[par], k), "hh", q_sb[:, :]).then_inc(c_ready, 1)
                for slot in {0: (1, 2), 1: (4, 5), 2: (7, 8), 3: (9, 10)}[k]:
                    fill(slot, pair, par, first, last_chunk, no_l2)
                pe.wait_ge(zh_done, n)
                project_twice(at_step(ps_r[npar], nk), "hr", zh_sb[:, :])
                pe.wait_ge(new_done, n)
                project(at_step(ps_r[npar], nk), "hr", new_sb[:, :]).then_inc(r_ready, 1)
                pe.wait_ge(hid_done, n + 1)
                project(at_step(ps_z[npar], nk), "hz", hid[:, par, k, :]).then_inc(z_ready, 1)
                t2 = k8 + 1 + LEAD
                if not last or k8 + 1 < 2 * STEPS - LEAD:
                    pe.wait_ge(h2_done, n)
                    project(at_step(ps_g, t2 % STEPS), "l2_h",
                            h2[:, (t2 - 1) // STEPS % 2, (t2 - 1) % STEPS, :]).then_inc(g_ready, 1)
                if k < STEPS - 1:
                    fill({0: 3, 1: 6, 2: 10}[k], pair, par, first, last_chunk, no_l2)
                else:
                    if not first:
                        pe.wait_ge(y_done, pair * 2 + par)
                    mm(ps_y, hid[:, par, :, :].rearrange("p s b -> p (s b)"), w("hq"), stop=False)

            pairs = CHUNKS // 2
            for k8 in range(2 * STEPS):
                step(0, k8, True, False)
            with pe.Fori(1, pairs - 1) as pair:
                for k8 in range(2 * STEPS):
                    step(pair, k8, False, False)
            for k8 in range(2 * STEPS):
                step(pairs - 1, k8, False, True)
            par = (CHUNKS - 1) % 2
            pe.wait_ge(hid_done, TIME + 1)
            pe.wait_ge(y_done, CHUNKS - 1)
            mm(ps_y, hid[:, par, :, :].rearrange("p s b -> p (s b)"), w("hq"), stop=False)
            mm(ps_y, x3[:, par, :], ident[:, :], start=False).then_inc(y_ready, 1)


def kernel(**inputs):
    import numpy as np
    import concourse.bacc as bacc
    from concourse.bass_utils import run_bass_kernel_spmd

    i = {k: np.asarray(v) for k, v in inputs.items()}
    n = N_STATE
    wp, l2w = i["L1_cond_Wp"], i["L2_cond_W"]
    twice = lambda a, axis: np.concatenate([a, a], axis=axis)
    squares = {
        "l0": i["L0_cond_weight"],
        "wp_b": twice(wp[:, :n], 1), "wp_c": twice(wp[:, n:], 1),
        "ws": twice(i["L1_cond_Ws"], 1), "wo": twice(i["L1_cond_Wo"], 0),
        "l2_h": l2w[:, :CH].T, "l2_z": l2w[:, CH:].T,
        "hr": i["L3_cond_Whr"].T, "hz": i["L3_cond_Whz"].T, "hh": i["L3_cond_Whh"].T,
        "xr": i["L3_cond_Wxr"].T, "xz": i["L3_cond_Wxz"].T, "xh": i["L3_cond_Wxh"].T,
        "hq": i["L3_cond_Whq"].T,
    }
    bp = i["L1_cond_bp"]
    columns = {
        "conv_b": i["L1_cond_conv_b"], "bp_b": twice(bp[:n], 0), "bp_c": twice(bp[n:], 0),
        "bs": twice(i["L1_cond_bs"], 0), "bo": i["L1_cond_bo"],
        "a_log": twice(i["L1_cond_A_log"], 0), "dt_log": twice(i["L1_cond_dt_log"], 0),
        "l2_b": i["L2_cond_b"], "alpha": i["L2_cond_alpha"],
        "bxr": i["L3_cond_bxr"], "bhr": i["L3_cond_bhr"], "bxz": i["L3_cond_bxz"],
        "bhz": i["L3_cond_bhz"], "bxh": i["L3_cond_bxh"], "bhh": i["L3_cond_bhh"],
    }
    arrays = {
        "x": np.ascontiguousarray(i["x"]),
        "cond": np.ascontiguousarray(i["cond_1024"]),
        "weights": np.ascontiguousarray(np.stack([squares[k] for k in WEIGHTS], axis=1)),
        "vectors": np.ascontiguousarray(np.stack([columns[k] for k in VECTORS], axis=1)),
        "bhq": np.ascontiguousarray(i["L3_cond_bhq"]),
    }
    nc = bacc.Bacc("TRN2", target_bir_lowering=False, num_devices=1)
    args = [nc.dram_tensor(k, a.shape, mybir.dt.from_np(a.dtype), kind="ExternalInput").ap()
            for k, a in arrays.items()]
    out = nc.dram_tensor("out", i["x"].shape, mybir.dt.float32, kind="ExternalOutput").ap()
    build(nc, *args, out)
    r = run_bass_kernel_spmd(nc, [arrays], core_ids=[0])
    return r.results[0]["out"]
```

```python
import concourse.bass as bass
from concourse import mybir
from contextlib import ExitStack

BATCH = 32
TIME = 128
CH = 128
N_STATE = 64
COLS = TIME * BATCH
STEPS = 4
CHUNK = STEPS * BATCH
CHUNKS = TIME // STEPS
BANK = 512
SLABS = COLS // BANK
BLOCK = 32
WINDOWS = TIME // BLOCK
WCOLS = BLOCK * BATCH
GROUPS = CH // BLOCK
ROWLEN = 2 * BLOCK
HALF_B = BATCH // 2
HALF_T = TIME // 2
FIRST_WEIGHTS = 4
X_PARTS = [(0, 8), (8, 16), (16, CHUNKS)]
LEAD = 6
EPS = 1e-8

WEIGHTS = ["l0", "ws", "wp_b", "wp_c", "wo", "l2_h", "l2_z",
           "hr", "hz", "hh", "xr", "xz", "xh", "hq"]
VECTORS = ["conv_b", "bp_b", "bp_c", "bs", "bo", "a_log", "dt_log", "l2_b", "alpha",
           "bxr", "bhr", "bxz", "bhz", "bxh", "bhh"]


def build(nc, x, cond, weights, vectors, bhq, out):
    f32 = mybir.dt.float32
    ACT = mybir.ActivationFunctionType
    ALU = mybir.AluOpType

    ctx = ExitStack()
    with ctx:
        def sb(name, shape):
            return ctx.enter_context(nc.sbuf_tensor(name, shape, f32))

        def sem(name):
            return ctx.enter_context(nc.semaphore(name))

        x_nat = sb("x_nat", [128, CHUNKS, CH])
        xT = sb("xT", [CH, COLS])
        xs = sb("xs", [CH, COLS])
        x1 = sb("x1", [CH, COLS])
        x1_win = sb("x1_win", [128, BLOCK, WINDOWS, BATCH])
        toep = sb("toep", [128, BLOCK, 2, 128])
        conv = sb("conv", [CH, COLS])
        soft = sb("soft", [128, TIME * HALF_B + 2])
        log_in = sb("log_in", [128, TIME * HALF_B + 2])
        u_sb = sb("u_sb", [128, TIME * HALF_B])
        gate_c = sb("gate_c", [128, TIME, HALF_B])
        decay_t = sb("decay_t", [128, HALF_B, HALF_T])
        room = toep[:, :, :, :].rearrange("p d v m -> p (d v m)")
        x2 = room[:, 0:COLS]
        third = TIME * HALF_B
        drive = room[:, COLS:COLS + third].rearrange("p (h b t) -> p h b t", h=2, b=HALF_B)
        state = room[:, COLS + third:COLS + 2 * third].rearrange("p (h b t) -> p h b t", h=2,
                                                                 b=HALF_B)
        gated = sb("gated", [128, TIME, HALF_B])
        w_sb = sb("w_sb", [128, len(WEIGHTS), 128])
        v_sb = sb("v_sb", [128, len(VECTORS)])
        bhq_rows = sb("bhq_rows", [128, CH])
        cond_nat = sb("cond_nat", [BATCH, CH])
        condT = sb("condT", [CH, BATCH])
        ysT = sb("ysT", [CH, BATCH])
        ys_sq = sb("ys_sq", [CH, BATCH])
        w0_sq = sb("w0_sq", [CH, CH])
        norm = sb("norm", [CH, 6, BATCH])
        dmod = sb("dmod", [CH, BATCH])
        filt = sb("filt", [CH, ROWLEN])
        filt_end = sb("filt_end", [1, ROWLEN])
        ident = sb("ident", [128, 128])
        flip = sb("flip", [BATCH, BATCH])
        ones = sb("ones", [128, BANK])
        proj_b = sb("proj_b", [128, 3])
        dt_a = sb("dt_a", [128, 2])
        leak = sb("leak", [CH, 1])
        gbias = sb("gbias", [CH, 3])
        dbias = sb("dbias", [CH, 4, CH])
        half = sb("half", [128, 1])
        warm = sb("warm", [128, 1])
        halved = sb("halved", [CH, 2, CH])
        z_sb = sb("z_sb", [CH, BATCH])
        q_sb = sb("q_sb", [CH, BATCH])
        zh_sb = sb("zh_sb", [CH, BATCH])
        omz_sb = sb("omz_sb", [CH, BATCH])
        new_sb = sb("new_sb", [CH, BATCH])
        hid = sb("hid", [CH, 2, STEPS, BATCH])
        g_sb = sb("g_sb", [CH, BATCH])
        gx_sb = sb("gx_sb", [CH, BATCH])
        s_sb = sb("s_sb", [CH, BATCH])
        h2 = sb("h2", [CH, 2, STEPS, BATCH])
        x3 = sb("x3", [CH, 2, CHUNK])
        y_sb = sb("y_sb", [128, 2, CH])

        filt_dram = nc.dram_tensor("filt_dram", [(CH + 1) * ROWLEN], f32, kind="Internal")

        ps = ctx.enter_context(nc.psum_tensor("ps", [128, 8, BANK], f32))
        ps_r = [ps[:, 0, 0:CHUNK], ps[:, 1, 0:CHUNK]]
        ps_z = [ps[:, 2, 0:CHUNK], ps[:, 3, 0:CHUNK]]
        ps_c = [ps[:, 4, 0:CHUNK], ps[:, 5, 0:CHUNK]]
        r_val = [ps[:, par, CHUNK:CHUNK + BATCH] for par in range(2)]
        cand_val = [ps[:, 4 + par, CHUNK:CHUNK + BATCH] for par in range(2)]
        ps_g = ps[:, 6, 0:CHUNK]
        ps_y = ps[:, 7, 0:CHUNK]
        SMALL = 7
        PROJ_B = 2
        BANK_U = [4, 5, 6, 7]
        BANK_B = [4, 5, 0, 1]
        BANK_C = [6, 7, 2, 3]
        BANK_Y = [(4, 5), (0, 1), (1, 3), (5, 7)]

        def w(name):
            return w_sb[:, WEIGHTS.index(name), :]

        def vec(name):
            k = VECTORS.index(name)
            return v_sb[:, k:k + 1]

        dt = soft[:, TIME * HALF_B + 1:TIME * HALF_B + 2]
        SOFT_AD = slice(TIME * HALF_B, TIME * HALF_B + 2)

        ZERO_DVE = 12
        XS_DVE = 4
        ADD_POOL = 2

        def wait_x1(engine, j):
            if j == 0:
                engine.wait_ge(x1_pool_done, ADD_POOL)
            else:
                engine.wait_ge(x1_done, 2 * (j + 1) - ADD_POOL)

        def win(j):
            return slice(j * BANK, (j + 1) * BANK)

        def bcast(t, n):
            return t[:, :].rearrange("p (o b) -> p o b", o=1).to_broadcast([CH, n, BATCH])

        def tb(t, lo, n):
            return t[:, lo:lo + n].rearrange("p (t b) -> p t b", b=BATCH)

        ld_cond, ld_w0, ld_w, ld_w_rest, ld_v, ld_bhq = (
            sem(n) for n in ("ld_cond", "ld_w0", "ld_w", "ld_w_rest", "ld_v", "ld_bhq"))
        ld_x = [sem("ld_x_%d" % part) for part in range(len(X_PARTS))]
        st_filt, ld_toep = sem("st_filt"), sem("ld_toep")
        toep_zero_dve, toep_zero_pool = sem("toep_zero_dve"), sem("toep_zero_pool")
        const_ready = sem("const_ready")
        cond_turned = sem("cond_turned")
        filt_done = sem("filt_done")
        ys_done, sq_done = sem("ys_done"), sem("sq_done")
        norm_mm, norm_in, norm_root, norm_step = (
            sem(n) for n in ("norm_mm", "norm_in", "norm_root", "norm_step"))
        x_turned, xT_done, xs_done, xs_pool_done, l0_mm, l0_scaled, x1_done, x1_pool_done = (
            sem(n) for n in ("x_turned", "xT_done", "xs_done", "xs_pool_done", "l0_mm",
                             "l0_scaled", "x1_done", "x1_pool_done"))
        win_done, conv_mm, conv_copied, conv_done = (
            sem(n) for n in ("win_done", "conv_mm", "conv_copied", "conv_done"))
        pb_mm, pb_done = sem("pb_mm"), sem("pb_done")
        relu_done, abs_act_done, abs_dve_done, tanh_done, log_done, soft_done = (
            sem(n) for n in ("relu_done", "abs_act_done", "abs_dve_done", "tanh_done", "log_done",
                             "soft_done"))
        decay_step, ad_relu, ad_abs, ad_tanh, ad_log = (
            sem(n) for n in ("decay_step", "ad_relu", "ad_abs", "ad_tanh", "ad_log"))
        u_mm, b_mm, c_mm, u_done = sem("u_mm"), sem("b_mm"), sem("c_mm"), sem("u_done")
        c_done = sem("c_done")
        carry_done = sem("carry_done")
        drive_done, scan_done, gated_done, y_mm, x2_done = (
            sem(n) for n in ("drive_done", "scan_done", "gated_done", "y_mm", "x2_done"))
        vec_done = sem("vec_done")
        pre_g, pre_sig, pre_gx, pre_s, pre_h = (
            sem(n) for n in ("pre_g", "pre_sig", "pre_gx", "pre_s", "pre_h"))
        r_ready, z_ready, c_ready, g_ready = (
            sem(n) for n in ("r_ready", "z_ready", "c_ready", "g_ready"))
        r_sig, z_sig, c_tanh, g_sig, h2_done = (
            sem(n) for n in ("r_sig", "z_sig", "c_tanh", "g_sig", "h2_done"))
        q_done, zh_done, omz_done, new_done, hid_done, gx_done, s_done = (
            sem(n) for n in ("q_done", "zh_done", "omz_done", "new_done", "hid_done", "gx_done",
                             "s_done"))
        x3_done, y_ready, y_done = sem("x3_done"), sem("y_ready"), sem("y_done")
        out_sent = [sem("out_sent_even"), sem("out_sent_odd")]

        out_v = out.rearrange("b (c s) d -> c s b d", s=STEPS)

        block = ctx.enter_context(nc.Block())

        @block.sync
        def _(sp_eng):
            sp_eng.dma_start(cond_nat[:, :], cond).then_inc(ld_cond, 16)
            x_v = x.rearrange("b (c s) d -> s b c d", s=STEPS)

            def load_x(part):
                first, after = X_PARTS[part]
                for s in range(STEPS):
                    sp_eng.dma_start(x_nat[s * BATCH:(s + 1) * BATCH, first:after, :],
                                     x_v[s, :, first:after, :]).then_inc(ld_x[part], 16)

            load_x(0)
            load_x(1)
            sp_eng.wait_ge(filt_done, 2)
            sp_eng.dma_start(filt_dram[0:CH * ROWLEN].rearrange("(d m) -> d m", m=ROWLEN),
                             filt[:, :]).then_inc(st_filt, 16)
            sp_eng.dma_start(filt_dram[CH * ROWLEN:(CH + 1) * ROWLEN].rearrange("(o m) -> o m", o=1),
                             filt_end[:, :]).then_inc(st_filt, 16)
            load_x(2)
            sp_eng.dma_start(w_sb[:, 1:FIRST_WEIGHTS, :],
                             weights[:, 1:FIRST_WEIGHTS, :]).then_inc(ld_w, 16)
            sp_eng.wait_ge(st_filt, 32)
            sp_eng.wait_ge(toep_zero_dve, 1)
            sp_eng.wait_ge(toep_zero_pool, 1)
            for g in range(GROUPS):
                src = bass.AP(filt_dram, g * BLOCK * ROWLEN,
                              [[1, BLOCK], [ROWLEN, BLOCK], [BLOCK, 2], [1, BLOCK]])
                rows = slice(g * BLOCK, (g + 1) * BLOCK)
                sp_eng.dma_start(toep[rows, :, :, rows], src).then_inc(ld_toep, 16)
            sp_eng.dma_start(w_sb[:, FIRST_WEIGHTS:, :],
                             weights[:, FIRST_WEIGHTS:, :]).then_inc(ld_w_rest, 16)
            sp_eng.dma_start(bhq_rows[:, :], bhq.rearrange("(o n) -> o n", o=1)
                             .to_broadcast([128, CH])).then_inc(ld_bhq, 16)

            def send(par, c):
                sp_eng.wait_ge(y_done, c + 1)
                sp_eng.dma_start(out_v[bass.ds(c, 1), :, :, :].rearrange("o s b d -> (o s) b d"),
                                 y_sb[:, par, :]).then_inc(out_sent[par], 16)

            with sp_eng.Fori(0, CHUNKS // 2) as pair:
                send(0, pair * 2)
                send(1, pair * 2 + 1)
            for par in range(2):
                sp_eng.wait_ge(out_sent[par], 16 * (CHUNKS // 2 + par))

        @block.gpsimd
        def _(pool):
            nc.gpsimd.memset(ident[:, :], 0.0).then_inc(const_ready, 1)
            nc.gpsimd.memset(flip[:, :], 0.0).then_inc(const_ready, 1)
            pool.wait_ge(const_ready, 2)
            nc.gpsimd.affine_select(out=ident[:, :], in_=ident[:, :], compare_op=ALU.not_equal,
                                    fill=1.0, base=0, pattern=[[-1, 128]],
                                    channel_multiplier=1).then_inc(const_ready, 1)
            nc.gpsimd.affine_select(out=flip[:, :], in_=flip[:, :], compare_op=ALU.not_equal,
                                    fill=1.0, base=1 - BATCH, pattern=[[1, BATCH]],
                                    channel_multiplier=1).then_inc(const_ready, 1)
            nc.gpsimd.memset(ones[:, :], 1.0).then_inc(const_ready, 1)
            nc.gpsimd.memset(filt[:, :], 0.0).then_inc(const_ready, 1)
            nc.gpsimd.memset(filt_end[:, :], 0.0).then_inc(const_ready, 1)
            nc.gpsimd.memset(half[:, :], 0.5).then_inc(const_ready, 1)
            nc.gpsimd.memset(decay_t[:, :, :], 1.0).then_inc(const_ready, 1)
            pool.wait_ge(const_ready, 9)
            nc.gpsimd.memset(decay_t[:, :, 0:1], 0.0).then_inc(const_ready, 1)
            nc.gpsimd.memset(toep[:, ZERO_DVE:, :, :], 0.0).then_inc(toep_zero_pool, 1)
            for q in range(ADD_POOL):
                cols = slice(q * BANK, (q + 1) * BANK)
                pool.wait_ge(l0_scaled, q + 1)
                nc.gpsimd.tensor_tensor(x1[:, cols], x1[:, cols], xT[:, cols],
                                        ALU.add).then_inc(x1_pool_done, 1)
            pool.wait_ge(ys_done, 2)
            for q in range(XS_DVE, SLABS):
                pool.wait_ge(xT_done, q + 1)
                nc.gpsimd.tensor_tensor(tb(xs, q * BANK, BANK), tb(xT, q * BANK, BANK),
                                        bcast(ysT, BANK // BATCH), ALU.mult).then_inc(xs_pool_done, 1)

        @block.scalar
        def _(act):
            act.dma_start(w_sb[:, 0, :], weights[:, 0, :]).then_inc(ld_w0, 16)
            act.dma_start(v_sb[:, :], vectors).then_inc(ld_v, 16)
            act.wait_ge(norm_in, 1)
            nc.scalar.activation(norm[:, 1, :], norm[:, 0, :], ACT.Sqrt).then_inc(norm_root, 1)
            k_log = VECTORS.index("a_log")
            log_pair = v_sb[:, k_log:k_log + 2]

            def decay_parts():
                nc.scalar.activation(soft[:, SOFT_AD], log_pair, ACT.Relu).then_inc(ad_relu, 1)
                nc.scalar.activation(log_in[:, SOFT_AD], log_pair, ACT.Abs).then_inc(ad_abs, 1)
                act.wait_ge(ad_abs, 1)
                nc.scalar.activation(log_in[:, SOFT_AD], log_in[:, SOFT_AD], ACT.Tanh,
                                     scale=0.5).then_inc(ad_tanh, 1)
                act.wait_ge(ad_tanh, 1)
                nc.scalar.activation(log_in[:, SOFT_AD], log_in[:, SOFT_AD], ACT.Ln,
                                     scale=0.5, bias=half[:, 0:1]).then_inc(ad_log, 1)
                nc.scalar.activation(warm[:, :], half[:, :], ACT.Tanh)

            def copy_u(j):
                act.wait_ge(u_mm, j + 1)
                nc.scalar.activation(u_sb[:, win(j)], ps[:, BANK_U[j], :], ACT.Identity,
                                     bias=vec("bs")).then_inc(u_done, 1)

            act.wait_ge(const_ready, 8)
            act.wait_ge(ld_v, 16)
            for q in range(SLABS):
                act.wait_ge(x_turned, q + 1)
                nc.scalar.activation(xT[:, q * BANK:(q + 1) * BANK], ps[:, q % 2, :],
                                     ACT.Copy).then_inc(xT_done, 1)
                if q == SLABS // 2 + 2:
                    copy_u(0)
            for j in range(1, WINDOWS):
                copy_u(j)
            decay_parts()

            def tanh_b(j):
                act.wait_ge(b_mm, j + 1)
                nc.scalar.activation(log_in[:, win(j)], ps[:, BANK_B[j], :], ACT.Tanh,
                                     bias=proj_b[:, 2:3], scale=0.5).then_inc(tanh_done, 1)

            def log_b(j):
                if j == 0:
                    act.wait_ge(abs_act_done, 1)
                else:
                    act.wait_ge(abs_dve_done, j)
                nc.scalar.activation(log_in[:, win(j)], log_in[:, win(j)], ACT.Ln,
                                     scale=0.5, bias=half[:, 0:1]).then_inc(log_done, 1)

            def tanh_c(j):
                act.wait_ge(c_mm, j + 1)
                nc.scalar.activation(gate_c[:, j * BLOCK:(j + 1) * BLOCK, :], ps[:, BANK_C[j], :]
                                     .rearrange("p (t b) -> p t b", b=HALF_B), ACT.Tanh,
                                     bias=proj_b[:, 1:2]).then_inc(c_done, 1)

            def lead_step(t):
                act.wait_ge(pre_g, t + 1)
                nc.scalar.activation(g_sb[:, :], ps_g[:, (t % STEPS) * BATCH:(t % STEPS + 1) * BATCH],
                                     ACT.Tanh, scale=0.5).then_inc(pre_sig, 1)
                act.wait_ge(pre_s, t + 1)
                nc.scalar.activation(h2[:, t // STEPS % 2, t % STEPS, :], s_sb[:, :],
                                     ACT.Tanh, scale=0.5).then_inc(pre_h, 1)

            for bank in range(SLABS):
                act.wait_ge(conv_mm, bank + 1)
                nc.scalar.activation(xs[:, bank * BANK:(bank + 1) * BANK], ps[:, bank, :],
                                     ACT.Copy).then_inc(conv_copied, 1)
            act.wait_ge(pb_done, 3)
            for j in range(WINDOWS):
                tanh_b(j)
                if j == 1:
                    act.wait_ge(tanh_done, 1)
                    nc.scalar.activation(log_in[:, win(0)], log_in[:, win(0)],
                                         ACT.Abs).then_inc(abs_act_done, 1)
            for j in range(WINDOWS):
                log_b(j)
            for j in range(WINDOWS):
                tanh_c(j)
            for t in range(LEAD):
                lead_step(t)

            def gates(n, k8, l2):
                par, k = k8 // STEPS, k8 % STEPS
                here = slice(k * BATCH, (k + 1) * BATCH)
                k2 = (k8 + LEAD) % STEPS
                act.wait_ge(r_ready, n)
                nc.scalar.activation(r_val[par], ps_r[par][:, here], ACT.Tanh,
                                     scale=0.5).then_inc(r_sig, 1)
                act.wait_ge(z_ready, n)
                nc.scalar.activation(z_sb[:, :], ps_z[par][:, here], ACT.Tanh,
                                     scale=0.5).then_inc(z_sig, 1)
                if l2:
                    act.wait_ge(g_ready, n)
                    nc.scalar.activation(g_sb[:, :], ps_g[:, k2 * BATCH:(k2 + 1) * BATCH],
                                         ACT.Tanh, scale=0.5).then_inc(g_sig, 1)

            def candidate(n, k8, l2):
                par, k = k8 // STEPS, k8 % STEPS
                here = slice(k * BATCH, (k + 1) * BATCH)
                par2, k2 = (k8 + LEAD) // STEPS % 2, (k8 + LEAD) % STEPS
                act.wait_ge(c_ready, n)
                nc.scalar.activation(cand_val[par], ps_c[par][:, here],
                                     ACT.Tanh).then_inc(c_tanh, 1)
                if l2:
                    act.wait_ge(s_done, n)
                    nc.scalar.activation(h2[:, par2, k2, :], s_sb[:, :], ACT.Tanh,
                                         scale=0.5).then_inc(h2_done, 1)

            pairs = CHUNKS // 2
            steps = 2 * STEPS
            gates(1, 0, True)
            with act.Fori(0, pairs - 1) as pair:
                for k8 in range(steps):
                    candidate(pair * steps + (k8 + 1), k8, True)
                    gates(pair * steps + (k8 + 2), (k8 + 1) % steps, True)
            for k8 in range(steps):
                candidate((pairs - 1) * steps + k8 + 1, k8, k8 < steps - LEAD)
                if k8 + 1 < steps:
                    gates((pairs - 1) * steps + k8 + 2, k8 + 1, k8 + 1 < steps - LEAD)

        @block.vector
        def _(dve):
            nc.vector.memset(toep[:, 0:ZERO_DVE, :, :], 0.0).then_inc(toep_zero_dve, 1)
            dve.wait_ge(cond_turned, 2)
            dve.wait_ge(const_ready, 7)
            nc.vector.tensor_copy(filt[:, BLOCK - 1:2 * BLOCK - 1],
                                  ps[:, SMALL, BATCH:2 * BATCH]).then_inc(filt_done, 2)
            nc.vector.tensor_copy(condT[:, :], ps[:, SMALL, 0:BATCH]).then_inc(ys_done, 1)
            nc.vector.tensor_scalar(ysT[:, :], ps[:, SMALL, 0:BATCH], float(CH) ** -0.5, None,
                                    ALU.mult).then_inc(ys_done, 1)
            dve.wait_ge(ys_done, 2)
            nc.vector.tensor_tensor(ys_sq[:, :], ysT[:, :], ysT[:, :], ALU.mult).then_inc(sq_done, 1)
            dve.wait_ge(ld_w0, 16)
            nc.vector.tensor_tensor(w0_sq[:, :], w("l0"), w("l0"), ALU.mult).then_inc(sq_done, 1)
            dve.wait_ge(norm_mm, 1)
            nc.vector.tensor_scalar(norm[:, 0, :], ps[:, SMALL, 2 * BATCH:3 * BATCH], EPS, None,
                                    ALU.add).then_inc(norm_in, 1)
            dve.wait_ge(norm_root, 1)
            nc.vector.reciprocal(norm[:, 2, :], norm[:, 1, :]).then_inc(norm_step, 1)
            dve.wait_ge(norm_step, 1)
            nc.vector.tensor_tensor(norm[:, 3, :], norm[:, 2, :], norm[:, 2, :],
                                    ALU.mult).then_inc(norm_step, 1)
            dve.wait_ge(norm_step, 2)
            nc.vector.tensor_tensor(norm[:, 4, :], norm[:, 3, :], norm[:, 0, :],
                                    ALU.mult).then_inc(norm_step, 1)
            dve.wait_ge(norm_step, 3)
            nc.vector.tensor_scalar(norm[:, 5, :], norm[:, 4, :], -0.5, 1.5, ALU.mult,
                                    ALU.add).then_inc(norm_step, 1)
            dve.wait_ge(norm_step, 4)
            nc.vector.tensor_tensor(dmod[:, :], norm[:, 2, :], norm[:, 5, :],
                                    ALU.mult).then_inc(norm_step, 1)
            dve.wait_ge(norm_step, 5)

            slab_t = BANK // BATCH

            def finish_x1(q):
                lo = q * BANK
                dve.wait_ge(l0_mm, q + 1)
                nc.vector.tensor_tensor(tb(x1, lo, BANK), ps[:, 2 + q % 2, :]
                                        .rearrange("p (t b) -> p t b", b=BATCH),
                                        bcast(dmod, slab_t), ALU.mult).then_inc(l0_scaled, 1)
                dve.wait_ge(l0_scaled, q + 1)
                if q >= ADD_POOL:
                    nc.vector.tensor_tensor(x1[:, lo:lo + BANK], x1[:, lo:lo + BANK],
                                            xT[:, lo:lo + BANK], ALU.add).then_inc(x1_done, 1)

            def window(j):
                wait_x1(dve, j)
                nc.vector.transpose(
                    x1_win[:, :, j, :].rearrange("p d b -> p b d"),
                    tb(x1, j * WCOLS, WCOLS)[:, ::-1, :].rearrange("p t b -> p b t")
                ).then_inc(win_done, 1)

            def scale_x(q):
                dve.wait_ge(xT_done, q + 1)
                nc.vector.tensor_tensor(tb(xs, q * BANK, BANK), tb(xT, q * BANK, BANK),
                                        bcast(ysT, slab_t), ALU.mult).then_inc(xs_done, 1)

            scale_x(0)
            for q in range(SLABS):
                if q + 1 < XS_DVE:
                    scale_x(q + 1)
                finish_x1(q)
                if q == 4:
                    window(0)
                if q == 6:
                    window(1)
            window(2)
            dve.wait_ge(ld_v, 16)
            dve.wait_ge(pb_mm, 2)
            nc.vector.tensor_tensor(proj_b[:, 0:1], ps[:, PROJ_B, 0:1], vec("bp_b"),
                                    ALU.add).then_inc(pb_done, 1)
            nc.vector.tensor_tensor(proj_b[:, 1:2], ps[:, PROJ_B, 1:2], vec("bp_c"),
                                    ALU.add).then_inc(pb_done, 1)
            window(3)
            dve.wait_ge(pb_done, 2)
            nc.vector.tensor_scalar(proj_b[:, 2:3], proj_b[:, 0:1], 0.5, None,
                                    ALU.mult).then_inc(pb_done, 1)
            dve.wait_ge(const_ready, 10)
            nc.vector.tensor_scalar(leak[:, :], vec("alpha"), -2.0, 2.0, ALU.mult,
                                    ALU.add).then_inc(vec_done, 1)
            for k, gate in enumerate(("r", "z", "h")):
                nc.vector.tensor_tensor(gbias[:, k:k + 1], vec("bx" + gate), vec("bh" + gate),
                                        ALU.add).then_inc(vec_done, 1)
            dve.wait_ge(vec_done, 4)
            for k in range(3):
                nc.vector.tensor_scalar(dbias[:, k, :], ident[:, :], gbias[:, k:k + 1], None,
                                        ALU.mult).then_inc(vec_done, 1)
            nc.vector.tensor_scalar(dbias[:, 3, :], ident[:, :], vec("l2_b"), None,
                                    ALU.mult).then_inc(vec_done, 1)
            def turn_back(j):
                dve.wait_ge(conv_copied, SLABS)
                src = xs[:, :].rearrange("p (m j b) -> p j b m", j=WINDOWS, b=BATCH)
                nc.vector.transpose(tb(conv, j * WCOLS, WCOLS).rearrange("p t b -> p b t"),
                                    src[:, j, :, :]).then_inc(conv_done, 1)

            def abs_b(j):
                dve.wait_ge(tanh_done, j + 1)
                nc.vector.scalar_tensor_tensor(
                    out=log_in[:, win(j)], in0=log_in[:, win(j)], scalar=-1.0,
                    in1=log_in[:, win(j)], op0=ALU.mult, op1=ALU.max).then_inc(abs_dve_done, 1)

            def relu_b(j):
                dve.wait_ge(tanh_done, j + 1)
                nc.vector.tensor_scalar(soft[:, win(j)], ps[:, BANK_B[j], :], proj_b[:, 0:1], 0.0,
                                        ALU.add, ALU.max).then_inc(relu_done, 1)

            def half_cols(j):
                return slice(j % 2 * BLOCK, (j % 2 + 1) * BLOCK)

            def soft_window(j):
                dve.wait_ge(log_done, j + 1)
                dve.wait_ge(relu_done, j + 1)
                nc.vector.tensor_tensor(soft[:, win(j)], soft[:, win(j)], log_in[:, win(j)],
                                        ALU.subtract).then_inc(soft_done, 1)

            def drive_window(j):
                dve.wait_ge(soft_done, j + 2)
                dve.wait_ge(u_done, j + 1)
                nc.vector.tensor_tensor(
                    drive[:, j // 2, :, half_cols(j)].rearrange("p b t -> p t b"),
                    u_sb[:, win(j)].rearrange("p (t b) -> p t b", b=HALF_B),
                    soft[:, win(j)].rearrange("p (t b) -> p t b", b=HALF_B),
                    ALU.mult).then_inc(drive_done, 1)

            def scan(h):
                dve.wait_ge(drive_done, 2 * (h + 1))
                if h == 1:
                    nc.vector.scalar_tensor_tensor(
                        out=drive[:, 1, :, 0:1], in0=state[:, 0, :, HALF_T - 1:HALF_T],
                        scalar=dt_a[:, 1:2], in1=drive[:, 1, :, 0:1],
                        op0=ALU.mult, op1=ALU.add).then_inc(carry_done, 1)
                    dve.wait_ge(carry_done, 1)
                nc.vector.tensor_tensor_scan(state[:, h, :, :].rearrange("p b t -> p (b t)"),
                                             decay_t[:, :, :].rearrange("p b t -> p (b t)"),
                                             drive[:, h, :, :].rearrange("p b t -> p (b t)"),
                                             0.0, ALU.mult, ALU.add).then_inc(scan_done, 1)

            def gate_window(j):
                dve.wait_ge(c_done, j + 1)
                dve.wait_ge(scan_done, j // 2 + 1)
                nc.vector.scalar_tensor_tensor(
                    out=gated[:, j * BLOCK:(j + 1) * BLOCK, :],
                    in0=state[:, j // 2, :, half_cols(j)].rearrange("p b t -> p t b"),
                    scalar=dt, in1=gate_c[:, j * BLOCK:(j + 1) * BLOCK, :],
                    op0=ALU.mult, op1=ALU.mult).then_inc(gated_done, 1)

            def x2_window(j):
                dve.wait_ge(y_mm, j + 1)
                for hb in range(2):
                    cols = slice(hb * HALF_B, (hb + 1) * HALF_B)
                    nc.vector.scalar_tensor_tensor(
                        out=tb(x2, j * WCOLS, WCOLS)[:, :, cols],
                        in0=ps[:, BANK_Y[j][hb], :].rearrange("p (t b) -> p t b", b=HALF_B),
                        scalar=vec("bo"), in1=tb(x1, j * WCOLS, WCOLS)[:, :, cols],
                        op0=ALU.add, op1=ALU.add).then_inc(x2_done, 1)

            def lead_step(t):
                dve.wait_ge(pre_sig, t + 1)
                nc.vector.scalar_tensor_tensor(
                    out=gx_sb[:, :], in0=g_sb[:, :], scalar=1.0, in1=x2[:, t * BATCH:(t + 1) * BATCH],
                    op0=ALU.add, op1=ALU.mult).then_inc(pre_gx, 1)
                dve.wait_ge(pre_gx, t + 1)
                nc.vector.scalar_tensor_tensor(
                    out=s_sb[:, :], in0=h2[:, (t - 1) // STEPS % 2, (t - 1) % STEPS, :],
                    scalar=leak[:, :], in1=gx_sb[:, :], op0=ALU.mult, op1=ALU.add
                ).then_inc(pre_s, 1)
                if t % STEPS == STEPS - 1:
                    c = t // STEPS
                    dve.wait_ge(pre_h, t + 2)
                    nc.vector.tensor_tensor(x3[:, c % 2, :], x2[:, c * CHUNK:(c + 1) * CHUNK],
                                            h2[:, c % 2, :, :].rearrange("p s b -> p (s b)"),
                                            ALU.add).then_inc(x3_done, 1)

            dve.wait_ge(ld_w_rest, 16)
            for k, name in enumerate(("hr", "hh")):
                nc.vector.tensor_scalar(halved[:, k, :], w(name), 0.5, None,
                                        ALU.mult).then_inc(vec_done, 1)
            dve.wait_ge(ad_log, 1)
            nc.vector.tensor_tensor(soft[:, SOFT_AD], soft[:, SOFT_AD], log_in[:, SOFT_AD],
                                    ALU.subtract).then_inc(soft_done, 1)
            dve.wait_ge(soft_done, 1)
            nc.vector.tensor_tensor(dt_a[:, 0:1], soft[:, SOFT_AD.start:SOFT_AD.start + 1], dt,
                                    ALU.mult).then_inc(decay_step, 1)
            dve.wait_ge(decay_step, 1)
            nc.vector.tensor_scalar(dt_a[:, 1:2], dt_a[:, 0:1], -1.0, 1.0, ALU.mult,
                                    ALU.add).then_inc(decay_step, 1)
            dve.wait_ge(decay_step, 2)
            nc.vector.tensor_scalar(decay_t[:, :, :], decay_t[:, :, :], dt_a[:, 1:2], None,
                                    ALU.mult).then_inc(decay_step, 1)
            dve.wait_ge(pb_done, 3)
            dve.wait_ge(decay_step, 3)
            for j in range(WINDOWS):
                turn_back(j)
            abs_b(1)
            relu_b(0)
            relu_b(1)
            abs_b(2)
            abs_b(3)
            dve.wait_ge(ys_done, 2)
            nc.vector.tensor_copy(h2[:, 1, STEPS - 1, :], condT[:, :]).then_inc(pre_h, 1)
            nc.vector.tensor_copy(hid[:, 1, STEPS - 1, :], condT[:, :]).then_inc(hid_done, 1)
            soft_window(0)
            drive_window(0)
            soft_window(1)
            drive_window(1)
            scan(0)
            gate_window(0)
            gate_window(1)
            relu_b(2)
            relu_b(3)
            soft_window(2)
            x2_window(0)
            drive_window(2)
            soft_window(3)
            drive_window(3)
            dve.wait_ge(pre_h, 1)
            dve.wait_ge(x2_done, 2)
            lead_step(0)
            x2_window(1)
            lead_step(1)
            scan(1)
            lead_step(2)
            gate_window(2)
            gate_window(3)
            lead_step(3)
            x2_window(2)
            lead_step(4)
            x2_window(3)
            lead_step(5)
            dve.wait_ge(x2_done, 2 * WINDOWS)
            dve.wait_ge(ld_bhq, 16)
            nc.vector.memset(y_sb[:, 1, :], 0.0).then_inc(out_sent[1], 16)

            def send_y(c, par, sent):
                if not isinstance(sent, int) or sent > 0:
                    dve.wait_ge(out_sent[par], sent)
                dve.wait_ge(y_ready, c + 1)
                nc.vector.tensor_tensor(y_sb[:, par, :], ps_y, bhq_rows[:, :],
                                        ALU.add).then_inc(y_done, 1)

            def step(n, t_off, k8, l2, out_chunk, out_count):
                par, k = k8 // STEPS, k8 % STEPS
                prev = hid[:, (k8 - 1) // STEPS % 2, (k8 - 1) % STEPS, :]
                t2 = k8 + LEAD
                par2, k2 = t2 // STEPS % 2, t2 % STEPS
                prev2 = h2[:, (t2 - 1) // STEPS % 2, (t2 - 1) % STEPS, :]
                dve.wait_ge(r_sig, n)
                dve.wait_ge(hid_done, n)
                nc.vector.scalar_tensor_tensor(out=q_sb[:, :], in0=r_val[par], scalar=1.0, in1=prev,
                                               op0=ALU.add, op1=ALU.mult).then_inc(q_done, 1)
                dve.wait_ge(z_sig, n)
                nc.vector.scalar_tensor_tensor(out=zh_sb[:, :], in0=z_sb[:, :], scalar=1.0, in1=prev,
                                               op0=ALU.add, op1=ALU.mult).then_inc(zh_done, 1)
                nc.vector.tensor_scalar(omz_sb[:, :], z_sb[:, :], -0.5, 0.5, ALU.mult,
                                        ALU.add).then_inc(omz_done, 1)
                if l2:
                    dve.wait_ge(g_sig, n)
                    col = t_off + (k8 + LEAD) * BATCH
                    nc.vector.scalar_tensor_tensor(
                        out=gx_sb[:, :], in0=g_sb[:, :], scalar=1.0, in1=x2[:, bass.ds(col, BATCH)],
                        op0=ALU.add, op1=ALU.mult).then_inc(gx_done, 1)
                dve.wait_ge(c_tanh, n)
                dve.wait_ge(omz_done, n)
                nc.vector.tensor_tensor(new_sb[:, :], omz_sb[:, :], cand_val[par],
                                        ALU.mult).then_inc(new_done, 1)
                if l2:
                    dve.wait_ge(gx_done, n)
                    nc.vector.scalar_tensor_tensor(out=s_sb[:, :], in0=prev2, scalar=leak[:, :],
                                                   in1=gx_sb[:, :], op0=ALU.mult,
                                                   op1=ALU.add).then_inc(s_done, 1)
                dve.wait_ge(new_done, n)
                nc.vector.scalar_tensor_tensor(out=hid[:, par, k, :], in0=zh_sb[:, :], scalar=0.5,
                                               in1=new_sb[:, :], op0=ALU.mult,
                                               op1=ALU.add).then_inc(hid_done, 1)
                if k == 1 and out_count is not None:
                    send_y(out_chunk, 1 - par, out_count)
                if l2 and k2 == STEPS - 1:
                    dve.wait_ge(h2_done, n)
                    lo = t_off + (k8 + LEAD - (STEPS - 1)) * BATCH
                    nc.vector.tensor_tensor(x3[:, par2, :], x2[:, bass.ds(lo, CHUNK)],
                                            h2[:, par2, :, :].rearrange("p s b -> p (s b)"),
                                            ALU.add).then_inc(x3_done, 1)

            pairs = CHUNKS // 2

            def chunk_pair(pair, peeled, last):
                for k8 in range(2 * STEPS):
                    par = k8 // STEPS
                    out_chunk = pair * 2 + (par - 1)
                    out_count = None if peeled and par == 0 else pair * 16
                    step(pair * (2 * STEPS) + (k8 + 1), pair * (2 * CHUNK), k8,
                         not last or k8 < 2 * STEPS - LEAD, out_chunk, out_count)

            chunk_pair(0, True, False)
            with dve.Fori(1, pairs - 1) as pair:
                chunk_pair(pair, False, False)
            chunk_pair(pairs - 1, False, True)
            send_y(CHUNKS - 1, 1, 16 * pairs)

        @block.tensor
        def _(pe):
            def mm(o, lhsT, rhs, start=True, stop=True):
                return nc.tensor.matmul(o, lhsT, rhs, start=start, stop=stop, skip_group_check=True)

            def keep_streaming(o, times=1):
                for _ in range(times):
                    mm(o, ident[:, :], ones[:, 0:o.shape[-1]])

            FREE = 4
            pe.wait_ge(const_ready, 5)
            keep_streaming(ps[:, FREE, 0:CHUNK], 3)
            pe.wait_ge(ld_cond, 16)
            nc.tensor.transpose(ps[:, SMALL, 0:BATCH], cond_nat[:, :],
                                ident[0:BATCH, 0:BATCH]).then_inc(cond_turned, 1)
            nc.tensor.transpose(ps[:, SMALL, BATCH:2 * BATCH], cond_nat[:, :],
                                flip[:, :]).then_inc(cond_turned, 1)
            keep_streaming(ps[:, FREE, 0:CHUNK], 3)
            pe.wait_ge(ys_done, 2)
            pe.wait_ge(sq_done, 2)
            mm(ps[:, SMALL, 2 * BATCH:3 * BATCH], w0_sq[:, :], ys_sq[:, :]).then_inc(norm_mm, 1)

            keep_streaming(ps[:, FREE, 0:CHUNK], 1)
            per = BANK // CHUNK

            def turn_x(q):
                for part, (first, after) in enumerate(X_PARTS):
                    if q * per == first:
                        pe.wait_ge(ld_x[part], 16 * STEPS)
                if q >= 2:
                    pe.wait_ge(xT_done, q - 1)
                for i in range(per):
                    last = nc.tensor.transpose(ps[:, q % 2, i * CHUNK:(i + 1) * CHUNK],
                                               x_nat[:, q * per + i, :], ident[:, :])
                last.then_inc(x_turned, 1)

            def l0(q):
                if q < XS_DVE:
                    pe.wait_ge(xs_done, q + 1)
                else:
                    pe.wait_ge(xs_pool_done, q + 1 - XS_DVE)
                if q >= 2:
                    pe.wait_ge(l0_scaled, q - 1)
                mm(ps[:, 2 + q % 2, :], w("l0"), xs[:, q * BANK:(q + 1) * BANK]).then_inc(l0_mm, 1)

            def conv_channel(i):
                bank, at = i // per, i % per * CHUNK
                rhs = x1_win[:, i, :, :].rearrange("p j b -> p (j b)")
                mm(ps[:, bank, at:at + CHUNK], toep[:, i, 0, :], rhs, stop=False)
                return mm(ps[:, bank, at + BATCH:at + CHUNK], toep[:, i, 1, :],
                          rhs[:, 0:(WINDOWS - 1) * BATCH], start=False)

            def batch_halves(name, src, j, bank, done):
                for hb in range(2):
                    rhs = tb(src, j * WCOLS, WCOLS)[:, :, hb * HALF_B:(hb + 1) * HALF_B]
                    last = mm(ps[hb * N_STATE:(hb + 1) * N_STATE, bank, :],
                              w(name)[:, 0:N_STATE], rhs)
                last.then_inc(done, 1)

            def project_u(j):
                wait_x1(pe, j)
                batch_halves("ws", x1, j, BANK_U[j], u_mm)

            def project_b(j):
                pe.wait_ge(conv_done, j + 1)
                batch_halves("wp_b", conv, j, BANK_B[j], b_mm)

            def project_c(j):
                batch_halves("wp_c", conv, j, BANK_C[j], c_mm)

            def project_y(j):
                pe.wait_ge(gated_done, j + 1)
                if j < 2:
                    pe.wait_ge(relu_done, 2 * (j + 1))
                elif j == 2:
                    pe.wait_ge(c_done, WINDOWS)
                    pe.wait_ge(x2_done, 4)
                for swap in range(2):
                    for hb in range(2):
                        rows = slice(hb * N_STATE, (hb + 1) * N_STATE)
                        outs = slice((hb ^ swap) * N_STATE, ((hb ^ swap) + 1) * N_STATE)
                        last = mm(ps[outs, BANK_Y[j][hb], :], w("wo")[rows, outs],
                                  gated[rows, j * BLOCK:(j + 1) * BLOCK, :]
                                  .rearrange("p t b -> p (t b)"))
                last.then_inc(y_mm, 1)

            turn_x(0)
            for q in range(SLABS):
                if q + 1 < SLABS:
                    turn_x(q + 1)
                if q == 4:
                    pe.wait_ge(ld_w, 16)
                    project_u(0)
                if q == 6:
                    project_u(1)
                l0(q)
                if q < 4:
                    keep_streaming(ps[:, FREE, 0:CHUNK], 1)
            project_u(2)
            pe.wait_ge(ld_v, 16)
            pe.wait_ge(l0_scaled, SLABS)
            for k, name in enumerate(("wp_b", "wp_c")):
                mm(ps[:, PROJ_B, k:k + 1], w(name), vec("conv_b")).then_inc(pb_mm, 1)
            project_u(3)
            keep_streaming(ps[:, 0, :], 1)

            pe.wait_ge(win_done, WINDOWS)
            pe.wait_ge(ld_toep, 16 * GROUPS)
            pe.wait_ge(u_done, WINDOWS)
            pe.wait_ge(pb_done, 2)
            for i in range(BLOCK):
                last = conv_channel(i)
                if i % per == per - 1:
                    last.then_inc(conv_mm, 1)
            pe.wait_ge(conv_copied, 1)
            keep_streaming(ps[:, 0, :], 2)
            for j in range(WINDOWS):
                project_b(j)
            for j in range(WINDOWS):
                project_c(j)
            pe.wait_ge(ld_w_rest, 16)
            pe.wait_ge(relu_done, 1)
            keep_streaming(ps[:, BANK_B[0], :], 5)
            project_y(0)
            project_y(1)

            DIAG = {"r": 0, "z": 1, "h": 2, "g": 3}

            def bias(o, gate):
                return mm(o, dbias[:, DIAG[gate], :], ones[:, 0:CHUNK], stop=False)

            def project(o, name, rhs):
                return mm(o, w(name), rhs, start=False)

            def project_twice(o, name, rhs):
                return mm(o, halved[:, ("hr", "hh").index(name), :], rhs, start=False)

            def at_step(o, k):
                return o[:, k * BATCH:(k + 1) * BATCH]

            pe.wait_ge(vec_done, 10)
            pe.wait_ge(c_done, 2)
            pe.wait_ge(x2_done, 2)

            def lead_chunk(t):
                if t:
                    pe.wait_ge(pre_sig, t)
                bias(ps_g, "g")
                project(ps_g, "l2_z", x2[:, t * BATCH:t * BATCH + CHUNK])

            def lead_step(t):
                pe.wait_ge(pre_h, t + 1)
                project(at_step(ps_g, t % STEPS), "l2_h",
                        h2[:, (t - 1) // STEPS % 2, (t - 1) % STEPS, :]).then_inc(pre_g, 1)

            spare = ps[:, 7, :]
            lead_chunk(0)
            lead_step(0)
            keep_streaming(spare, 1)
            lead_step(1)
            pe.wait_ge(c_done, WINDOWS)
            bias(ps_z[0], "z")
            bias(ps_c[0], "h")
            keep_streaming(spare, 1)
            lead_step(2)
            keep_streaming(spare, 1)
            pe.wait_ge(x2_done, 4)
            bias(ps_r[0], "r")
            lead_step(3)
            lead_chunk(STEPS)
            project_y(2)
            lead_step(4)
            project_y(3)
            lead_step(5)
            pe.wait_ge(x3_done, 1)
            for gate, o in (("r", ps_r), ("z", ps_z), ("h", ps_c)):
                project(o[0], "x" + gate, x3[:, 0, :])

            pe.wait_ge(hid_done, 1)
            h_init = hid[:, 1, STEPS - 1, :]
            project(at_step(ps_r[0], 0), "hr", h_init).then_inc(r_ready, 1)
            project(at_step(ps_z[0], 0), "hz", h_init).then_inc(z_ready, 1)
            pe.wait_ge(pre_h, LEAD + 1)
            project(at_step(ps_g, LEAD % STEPS), "l2_h",
                    h2[:, (LEAD - 1) // STEPS % 2, (LEAD - 1) % STEPS, :]).then_inc(g_ready, 1)
            pe.wait_ge(x2_done, 2 * WINDOWS)
            keep_streaming(ps[:, 1, :], 2)

            def fill(slot, pair, par, first, last_chunk, no_l2):
                nxt = 1 - par
                if slot == 1 and not first:
                    mm(ps_y, x3[:, nxt, :], ident[:, :], start=False).then_inc(y_ready, 1)
                elif slot > 9 or last_chunk or slot == 1 or (slot in (4, 5) and no_l2):
                    if slot > 9 and not last_chunk:
                        if not first:
                            pe.wait_ge(y_done, pair * 2 + par)
                        keep_streaming(ps_y)
                    else:
                        keep_streaming(ps_c[nxt])
                if last_chunk:
                    return
                if slot == 2:
                    bias(ps_r[nxt], "r")
                if slot == 3:
                    bias(ps_z[nxt], "z")
                if slot == 4 and not no_l2:
                    pe.wait_ge(g_sig, pair * (2 * STEPS) + (par * STEPS + 2))
                    bias(ps_g, "g")
                if slot == 5 and not no_l2:
                    lo = pair * (2 * CHUNK) + (par + 2) * CHUNK
                    project(ps_g, "l2_z", x2[:, bass.ds(lo, CHUNK)])
                if slot == 6:
                    bias(ps_c[nxt], "h")
                if slot == 7:
                    pe.wait_ge(x3_done, pair * 2 + (par + 2))
                    project(ps_r[nxt], "xr", x3[:, nxt, :])
                if slot == 8:
                    project(ps_z[nxt], "xz", x3[:, nxt, :])
                if slot == 9:
                    project(ps_c[nxt], "xh", x3[:, nxt, :])

            def step(pair, k8, peeled, last):
                par, k = k8 // STEPS, k8 % STEPS
                n = pair * (2 * STEPS) + (k8 + 1)
                first = peeled and par == 0
                last_chunk = last and par == 1
                no_l2 = last
                nxt8 = (k8 + 1) % (2 * STEPS)
                npar, nk = nxt8 // STEPS, nxt8 % STEPS
                if last and k8 == 2 * STEPS - 1:
                    pe.wait_ge(q_done, n)
                    project_twice(at_step(ps_c[par], k), "hh", q_sb[:, :]).then_inc(c_ready, 1)
                    return
                pe.wait_ge(q_done, n)
                project_twice(at_step(ps_c[par], k), "hh", q_sb[:, :]).then_inc(c_ready, 1)
                for slot in {0: (1, 2), 1: (4, 5), 2: (7, 8), 3: (9, 10)}[k]:
                    fill(slot, pair, par, first, last_chunk, no_l2)
                pe.wait_ge(zh_done, n)
                project_twice(at_step(ps_r[npar], nk), "hr", zh_sb[:, :])
                pe.wait_ge(new_done, n)
                project(at_step(ps_r[npar], nk), "hr", new_sb[:, :]).then_inc(r_ready, 1)
                pe.wait_ge(hid_done, n + 1)
                project(at_step(ps_z[npar], nk), "hz", hid[:, par, k, :]).then_inc(z_ready, 1)
                t2 = k8 + 1 + LEAD
                if not last or k8 + 1 < 2 * STEPS - LEAD:
                    pe.wait_ge(h2_done, n)
                    project(at_step(ps_g, t2 % STEPS), "l2_h",
                            h2[:, (t2 - 1) // STEPS % 2, (t2 - 1) % STEPS, :]).then_inc(g_ready, 1)
                if k < STEPS - 1:
                    fill({0: 3, 1: 6, 2: 10}[k], pair, par, first, last_chunk, no_l2)
                else:
                    if not first:
                        pe.wait_ge(y_done, pair * 2 + par)
                    mm(ps_y, hid[:, par, :, :].rearrange("p s b -> p (s b)"), w("hq"), stop=False)

            pairs = CHUNKS // 2
            for k8 in range(2 * STEPS):
                step(0, k8, True, False)
            with pe.Fori(1, pairs - 1) as pair:
                for k8 in range(2 * STEPS):
                    step(pair, k8, False, False)
            for k8 in range(2 * STEPS):
                step(pairs - 1, k8, False, True)
            par = (CHUNKS - 1) % 2
            pe.wait_ge(hid_done, TIME + 1)
            pe.wait_ge(y_done, CHUNKS - 1)
            mm(ps_y, hid[:, par, :, :].rearrange("p s b -> p (s b)"), w("hq"), stop=False)
            mm(ps_y, x3[:, par, :], ident[:, :], start=False).then_inc(y_ready, 1)


def kernel(**inputs):
    import numpy as np
    import concourse.bacc as bacc
    from concourse.bass_utils import run_bass_kernel_spmd

    i = {k: np.asarray(v) for k, v in inputs.items()}
    n = N_STATE
    wp, l2w = i["L1_cond_Wp"], i["L2_cond_W"]
    twice = lambda a, axis: np.concatenate([a, a], axis=axis)
    squares = {
        "l0": i["L0_cond_weight"],
        "wp_b": twice(wp[:, :n], 1), "wp_c": twice(wp[:, n:], 1),
        "ws": twice(i["L1_cond_Ws"], 1), "wo": twice(i["L1_cond_Wo"], 0),
        "l2_h": l2w[:, :CH].T, "l2_z": l2w[:, CH:].T,
        "hr": i["L3_cond_Whr"].T, "hz": i["L3_cond_Whz"].T, "hh": i["L3_cond_Whh"].T,
        "xr": i["L3_cond_Wxr"].T, "xz": i["L3_cond_Wxz"].T, "xh": i["L3_cond_Wxh"].T,
        "hq": i["L3_cond_Whq"].T,
    }
    bp = i["L1_cond_bp"]
    columns = {
        "conv_b": i["L1_cond_conv_b"], "bp_b": twice(bp[:n], 0), "bp_c": twice(bp[n:], 0),
        "bs": twice(i["L1_cond_bs"], 0), "bo": i["L1_cond_bo"],
        "a_log": twice(i["L1_cond_A_log"], 0), "dt_log": twice(i["L1_cond_dt_log"], 0),
        "l2_b": i["L2_cond_b"], "alpha": i["L2_cond_alpha"],
        "bxr": i["L3_cond_bxr"], "bhr": i["L3_cond_bhr"], "bxz": i["L3_cond_bxz"],
        "bhz": i["L3_cond_bhz"], "bxh": i["L3_cond_bxh"], "bhh": i["L3_cond_bhh"],
    }
    arrays = {
        "x": np.ascontiguousarray(i["x"]),
        "cond": np.ascontiguousarray(i["cond_1024"]),
        "weights": np.ascontiguousarray(np.stack([squares[k] for k in WEIGHTS], axis=1)),
        "vectors": np.ascontiguousarray(np.stack([columns[k] for k in VECTORS], axis=1)),
        "bhq": np.ascontiguousarray(i["L3_cond_bhq"]),
    }
    nc = bacc.Bacc("TRN2", target_bir_lowering=False, num_devices=1)
    args = [nc.dram_tensor(k, a.shape, mybir.dt.from_np(a.dtype), kind="ExternalInput").ap()
            for k, a in arrays.items()]
    out = nc.dram_tensor("out", i["x"].shape, mybir.dt.float32, kind="ExternalOutput").ap()
    build(nc, *args, out)
    r = run_bass_kernel_spmd(nc, [arrays], core_ids=[0])
    return r.results[0]["out"]
```
